# Optimizing a Trainium2 kernel written in Bass

```python
import numpy as np
import jax
import jax.numpy as jnp

def _softmax(x, axis=-1):
    return jax.nn.softmax(x, axis=axis)

def _gelu(x):
    return jax.nn.gelu(x, approximate=True)

def _silu(x):
    return jax.nn.silu(x)

def _sigmoid(x):
    return jax.nn.sigmoid(x)

def _layernorm(x, axis=-1, eps=1e-05):
    m = jnp.mean(x, axis=axis, keepdims=True)
    v = jnp.var(x, axis=axis, keepdims=True)
    return (x - m) / jnp.sqrt(v + eps)

def _scatter_add(tgt, idx, src, axis=0):
    return tgt.at[idx].add(src)

def _segment_sum(src, seg, n):
    return jax.ops.segment_sum(src, seg, n)
kernel_name = 'mk_gnn_resnorm_d4_gnn_r32_523c3a'

def setup_inputs(seed: int=0):
    np.random.seed(seed)
    _w = jnp.asarray

    def _rec_inputs():
        import jax
        import jax.numpy as jnp
        _gk = jax.random.key(seed)
        x = -0.0008691 + 1 * jax.random.normal(jax.random.fold_in(_gk, 1), (3125, 128), jnp.float32)
        _s = jax.random.randint(jax.random.fold_in(_gk, 2), (25000,), 0, 3125, jnp.int32)
        _d = jax.random.randint(jax.random.fold_in(_gk, 3), (25000,), 0, 3125, jnp.int32)
        _loop = jnp.arange(3125, dtype=jnp.int32)
        src = jnp.concatenate([_s, _d, _loop])
        dst = jnp.concatenate([_d, _s, _loop])
        _o = jnp.argsort(dst, stable=True)
        src = src[_o]
        dst = dst[_o]
        edge_attr_128 = 5.93493e-05 + 1.00006 * jax.random.normal(jax.random.fold_in(_gk, 11), (53125, 128), jnp.float32)
        edge_type_2 = jax.random.randint(jax.random.fold_in(_gk, 13), (53125,), 0, 2, jnp.int32)
        edge_type_9 = jax.random.randint(jax.random.fold_in(_gk, 14), (53125,), 0, 9, jnp.int32)
        return (x, src, dst, edge_attr_128, edge_type_2, edge_type_9)
    x, src, dst, edge_attr_128, edge_type_2, edge_type_9 = _rec_inputs()

    def _L0_gnn_setup():
        import jax, jax.numpy as jnp
        import numpy as np
        N_NODES = 10000
        N_EDGES = 20000
        D = 128
        MEM = 128

        def _gru_step(x_t, w_ih, w_hh, b_ih, b_hh):
            H = x_t.shape[-1]
            gi = x_t @ w_ih.T + b_ih
            gh = jnp.broadcast_to(b_hh, gi.shape)
            i_r, i_z, i_n = (gi[:, :H], gi[:, H:2 * H], gi[:, 2 * H:])
            h_r, h_z, h_n = (gh[:, :H], gh[:, H:2 * H], gh[:, 2 * H:])
            r = jax.nn.sigmoid(i_r + h_r)
            z = jax.nn.sigmoid(i_z + h_z)
            n = jnp.tanh(i_n + r * h_n)
            return (1.0 - z) * n
        key = jax.random.key(seed)
        ks = jax.random.split(key, 10)
        s = 1.0 / np.sqrt(MEM)
        return {'x': jax.random.normal(ks[0], (N_NODES, D), dtype=jnp.float32), 'edge_index': jax.random.randint(ks[1], (2, N_EDGES), 0, N_NODES, dtype=jnp.int64), 'memory': jax.random.normal(ks[2], (1, MEM), dtype=jnp.float32), 'gru_w_ih': jax.random.uniform(ks[3], (3 * MEM, MEM), jnp.float32, -s, s), 'gru_w_hh': jax.random.uniform(ks[4], (3 * MEM, MEM), jnp.float32, -s, s), 'gru_b_ih': jax.random.uniform(ks[5], (3 * MEM,), jnp.float32, -s, s), 'gru_b_hh': jax.random.uniform(ks[6], (3 * MEM,), jnp.float32, -s, s), 'wt_w': jax.random.uniform(ks[7], (D * D, MEM), jnp.float32, -s, s), 'wt_b': jax.random.uniform(ks[8], (D * D,), jnp.float32, -s, s), 'lin_b': jax.random.uniform(ks[9], (D,), jnp.float32, -s, s)}
    _L0_gnn_all = _L0_gnn_setup()
    _L0_gnn_in = {k: v for k, v in _L0_gnn_all.items() if k in ('memory', 'gru_w_ih', 'gru_w_hh', 'gru_b_ih', 'gru_b_hh', 'wt_w', 'wt_b', 'lin_b')}
    del _L0_gnn_all

    def _L1_gnn_setup():
        import jax, jax.numpy as jnp
        import numpy as np
        IN_DIM = 128
        OUT_DIM = 128
        N_NODES = 10000
        N_EDGES = 20000
        key = jax.random.key(seed)
        ks = jax.random.split(key, 9)
        X = jax.random.normal(ks[0], (N_NODES, IN_DIM), dtype=jnp.float32)
        edge_index = jax.random.randint(ks[1], (2, N_EDGES), 0, N_NODES, dtype=jnp.int64)
        edge_types = jax.random.randint(ks[2], (N_EDGES,), 0, 2, dtype=jnp.int64)
        s = 1.0 / np.sqrt(IN_DIM)
        W_data = jax.random.uniform(ks[3], (OUT_DIM, IN_DIM), minval=-s, maxval=s, dtype=jnp.float32)
        b_data = jax.random.uniform(ks[4], (OUT_DIM,), minval=-s, maxval=s, dtype=jnp.float32)
        W_control = jax.random.uniform(ks[5], (OUT_DIM, IN_DIM), minval=-s, maxval=s, dtype=jnp.float32)
        b_control = jax.random.uniform(ks[6], (OUT_DIM,), minval=-s, maxval=s, dtype=jnp.float32)
        W_self = jax.random.uniform(ks[7], (OUT_DIM, IN_DIM), minval=-s, maxval=s, dtype=jnp.float32)
        b_self = jax.random.uniform(ks[8], (OUT_DIM,), minval=-s, maxval=s, dtype=jnp.float32)
        return {'X': X, 'edge_index': edge_index, 'edge_types': edge_types, 'W_data': W_data, 'b_data': b_data, 'W_control': W_control, 'b_control': b_control, 'W_self': W_self, 'b_self': b_self}
    _L1_gnn_all = _L1_gnn_setup()
    _L1_gnn_in = {k: v for k, v in _L1_gnn_all.items() if k in ('W_data', 'b_data', 'W_control', 'b_control', 'W_self', 'b_self')}
    del _L1_gnn_all

    def _L2_gnn_setup():
        import jax, jax.numpy as jnp
        import numpy as np
        N_NODES = 50000
        N_EDGES = 18750
        D = 128
        NUM_LAYERS = 2
        ALPHA = 0.5

        def _l2norm(v, axis):
            n = jnp.sqrt(jnp.sum(v * v, axis=axis, keepdims=True))
            return v / jnp.maximum(n, 1e-12)
        key = jax.random.key(seed)
        k1, k2, k3, k4 = jax.random.split(key, 4)
        x = jax.random.normal(k1, (N_NODES, D), dtype=jnp.float32)
        edge_index = jax.random.randint(k2, (2, N_EDGES), 0, N_NODES, dtype=jnp.int64)
        edge_attr = jax.random.normal(k3, (N_EDGES, D), dtype=jnp.float32)
        question_emb = jax.random.normal(k4, (1, D), dtype=jnp.float32)
        return {'x': x, 'edge_index': edge_index, 'edge_attr': edge_attr, 'question_emb': question_emb}
    _L2_gnn_all = _L2_gnn_setup()
    _L2_gnn_in = {k: v for k, v in _L2_gnn_all.items() if k in ('question_emb',)}
    del _L2_gnn_all

    def _L3_gnn_setup():
        import jax, jax.numpy as jnp
        import numpy as np
        NUM_EDGE_TYPES = 8
        HIDDEN = 128
        N_NODES = 50000
        N_EDGES = 18750

        def _gru_cell(x, h, W_ih, W_hh, b_ih, b_hh):
            H = h.shape[-1]
            gi = x @ W_ih.T + b_ih
            gh = h @ W_hh.T + b_hh
            i_r, i_z, i_n = (gi[:, :H], gi[:, H:2 * H], gi[:, 2 * H:])
            h_r, h_z, h_n = (gh[:, :H], gh[:, H:2 * H], gh[:, 2 * H:])
            r = jax.nn.sigmoid(i_r + h_r)
            z = jax.nn.sigmoid(i_z + h_z)
            n = jnp.tanh(i_n + r * h_n)
            return (1.0 - z) * n + z * h
        key = jax.random.key(seed)
        ks = jax.random.split(key, 10)
        H = HIDDEN
        h = jax.random.normal(ks[0], (N_NODES, H), dtype=jnp.float32)
        edge_index = jax.random.randint(ks[1], (2, N_EDGES), 0, N_NODES, dtype=jnp.int32)
        edge_type = jax.random.randint(ks[2], (N_EDGES,), 0, NUM_EDGE_TYPES + 1, dtype=jnp.int32)
        s = 1.0 / np.sqrt(H)
        W_msg = jax.random.uniform(ks[3], (H, H), jnp.float32, -s, s)
        b_msg = jax.random.uniform(ks[4], (H,), jnp.float32, -s, s)
        edge_embed = jax.random.normal(ks[5], (NUM_EDGE_TYPES + 1, H), dtype=jnp.float32)
        W_ih = jax.random.uniform(ks[6], (3 * H, H), jnp.float32, -s, s)
        W_hh = jax.random.uniform(ks[7], (3 * H, H), jnp.float32, -s, s)
        b_ih = jax.random.uniform(ks[8], (3 * H,), jnp.float32, -s, s)
        b_hh = jax.random.uniform(ks[9], (3 * H,), jnp.float32, -s, s)
        return {'h': h, 'edge_index': edge_index, 'edge_type': edge_type, 'num_nodes': N_NODES, 'W_msg': W_msg, 'b_msg': b_msg, 'edge_embed': edge_embed, 'W_ih': W_ih, 'W_hh': W_hh, 'b_ih': b_ih, 'b_hh': b_hh}
    _L3_gnn_all = _L3_gnn_setup()
    _L3_gnn_in = {k: v for k, v in _L3_gnn_all.items() if k in ('W_msg', 'b_msg', 'edge_embed', 'W_ih', 'W_hh', 'b_ih', 'b_hh')}
    del _L3_gnn_all
    return {'x': x, 'src': src, 'dst': dst, 'edge_attr_128': edge_attr_128, 'edge_type_2': edge_type_2, 'edge_type_9': edge_type_9, 'L0_gnn_memory': _L0_gnn_in['memory'], 'L0_gnn_gru_w_ih': _L0_gnn_in['gru_w_ih'], 'L0_gnn_gru_w_hh': _L0_gnn_in['gru_w_hh'], 'L0_gnn_gru_b_ih': _L0_gnn_in['gru_b_ih'], 'L0_gnn_gru_b_hh': _L0_gnn_in['gru_b_hh'], 'L0_gnn_wt_w': _L0_gnn_in['wt_w'], 'L0_gnn_wt_b': _L0_gnn_in['wt_b'], 'L0_gnn_lin_b': _L0_gnn_in['lin_b'], 'L1_gnn_W_data': _L1_gnn_in['W_data'], 'L1_gnn_b_data': _L1_gnn_in['b_data'], 'L1_gnn_W_control': _L1_gnn_in['W_control'], 'L1_gnn_b_control': _L1_gnn_in['b_control'], 'L1_gnn_W_self': _L1_gnn_in['W_self'], 'L1_gnn_b_self': _L1_gnn_in['b_self'], 'L2_gnn_question_emb': _L2_gnn_in['question_emb'], 'L3_gnn_W_msg': _L3_gnn_in['W_msg'], 'L3_gnn_b_msg': _L3_gnn_in['b_msg'], 'L3_gnn_edge_embed': _L3_gnn_in['edge_embed'], 'L3_gnn_W_ih': _L3_gnn_in['W_ih'], 'L3_gnn_W_hh': _L3_gnn_in['W_hh'], 'L3_gnn_b_ih': _L3_gnn_in['b_ih'], 'L3_gnn_b_hh': _L3_gnn_in['b_hh']}

def reference(x, src, dst, edge_attr_128, edge_type_2, edge_type_9, L0_gnn_memory, L0_gnn_gru_w_ih, L0_gnn_gru_w_hh, L0_gnn_gru_b_ih, L0_gnn_gru_b_hh, L0_gnn_wt_w, L0_gnn_wt_b, L0_gnn_lin_b, L1_gnn_W_data, L1_gnn_b_data, L1_gnn_W_control, L1_gnn_b_control, L1_gnn_W_self, L1_gnn_b_self, L2_gnn_question_emb, L3_gnn_W_msg, L3_gnn_b_msg, L3_gnn_edge_embed, L3_gnn_W_ih, L3_gnn_W_hh, L3_gnn_b_ih, L3_gnn_b_hh):
    import jax
    import jax.numpy as jnp

    def _L0_gnn_ref(x, edge_index, memory, gru_w_ih, gru_w_hh, gru_b_ih, gru_b_hh, wt_w, wt_b, lin_b):
        import jax, jax.numpy as jnp
        import numpy as np
        N_NODES = 10000
        N_EDGES = 20000
        D = 128
        MEM = 128

        def _gru_step(x_t, w_ih, w_hh, b_ih, b_hh):
            H = x_t.shape[-1]
            gi = x_t @ w_ih.T + b_ih
            gh = jnp.broadcast_to(b_hh, gi.shape)
            i_r, i_z, i_n = (gi[:, :H], gi[:, H:2 * H], gi[:, 2 * H:])
            h_r, h_z, h_n = (gh[:, :H], gh[:, H:2 * H], gh[:, 2 * H:])
            r = jax.nn.sigmoid(i_r + h_r)
            z = jax.nn.sigmoid(i_z + h_z)
            n = jnp.tanh(i_n + r * h_n)
            return (1.0 - z) * n
        update_memory = _gru_step(memory, gru_w_ih, gru_w_hh, gru_b_ih, gru_b_hh)[0]
        new_w = (update_memory @ wt_w.T + wt_b).reshape(lin_b.shape[0], x.shape[1])
        new_w = jax.lax.stop_gradient(new_w)
        src, dst = (edge_index[0], edge_index[1])
        agg = jax.ops.segment_sum(x[src], dst, num_segments=x.shape[0])
        h = x + agg
        return jax.nn.relu(h @ new_w.T + lin_b)

    def _L1_gnn_ref(X, edge_index, edge_types, W_data, b_data, W_control, b_control, W_self, b_self):
        import jax, jax.numpy as jnp
        import numpy as np
        IN_DIM = 128
        OUT_DIM = 128
        N_NODES = 10000
        N_EDGES = 20000
        src, dst = (edge_index[0], edge_index[1])
        Xs = X[src]
        m_data = Xs @ W_data.T + b_data
        m_ctrl = Xs @ W_control.T + b_control
        msg = jnp.where((edge_types == 0)[:, None], m_data, m_ctrl)
        agg = jax.ops.segment_sum(msg, dst, num_segments=X.shape[0])
        out = agg + (X @ W_self.T + b_self)
        return jax.nn.relu(out)

    def _L2_gnn_ref(x, edge_index, edge_attr, question_emb):
        import jax, jax.numpy as jnp
        import numpy as np
        N_NODES = 50000
        N_EDGES = 18750
        D = 128
        NUM_LAYERS = 2
        ALPHA = 0.5

        def _l2norm(v, axis):
            n = jnp.sqrt(jnp.sum(v * v, axis=axis, keepdims=True))
            return v / jnp.maximum(n, 1e-12)
        num_nodes = x.shape[0]
        src, dst = (edge_index[0], edge_index[1])
        q = _l2norm(question_emb[0], axis=0)
        edge_sim = _l2norm(edge_attr, axis=1) @ q
        deg = jax.ops.segment_sum(jnp.ones_like(edge_sim), dst, num_segments=num_nodes)
        deg = jnp.maximum(deg, 1.0)[:, None]
        for _ in range(NUM_LAYERS):
            msgs = x[src] * edge_sim[:, None]
            x_new = jax.ops.segment_sum(msgs, dst, num_segments=num_nodes)
            x_new = x_new / deg
            x = ALPHA * x + (1.0 - ALPHA) * x_new
        return x

    def _L3_gnn_ref(h, edge_index, edge_type, num_nodes, W_msg, b_msg, edge_embed, W_ih, W_hh, b_ih, b_hh):
        import jax, jax.numpy as jnp
        import numpy as np
        NUM_EDGE_TYPES = 8
        HIDDEN = 128
        N_NODES = 50000
        N_EDGES = 18750

        def _gru_cell(x, h, W_ih, W_hh, b_ih, b_hh):
            H = h.shape[-1]
            gi = x @ W_ih.T + b_ih
            gh = h @ W_hh.T + b_hh
            i_r, i_z, i_n = (gi[:, :H], gi[:, H:2 * H], gi[:, 2 * H:])
            h_r, h_z, h_n = (gh[:, :H], gh[:, H:2 * H], gh[:, 2 * H:])
            r = jax.nn.sigmoid(i_r + h_r)
            z = jax.nn.sigmoid(i_z + h_z)
            n = jnp.tanh(i_n + r * h_n)
            return (1.0 - z) * n + z * h
        src = edge_index[0]
        dst = edge_index[1]
        src_h = h[src] @ W_msg.T + b_msg
        emb = edge_embed[jnp.clip(edge_type, 0, NUM_EDGE_TYPES)]
        msg = src_h + emb
        messages = jax.ops.segment_sum(msg, dst, num_segments=num_nodes)
        h_new = _gru_cell(messages, h[:num_nodes], W_ih, W_hh, b_ih, b_hh)
        result = jnp.zeros_like(h).at[:num_nodes].set(h_new)
        return result
    edge_index = jnp.stack([src, dst])
    x = _layernorm(x + _L0_gnn_ref(x, edge_index, L0_gnn_memory, L0_gnn_gru_w_ih, L0_gnn_gru_w_hh, L0_gnn_gru_b_ih, L0_gnn_gru_b_hh, L0_gnn_wt_w, L0_gnn_wt_b, L0_gnn_lin_b), axis=-1)
    x = _layernorm(x + _L1_gnn_ref(x, edge_index, edge_type_2, L1_gnn_W_data, L1_gnn_b_data, L1_gnn_W_control, L1_gnn_b_control, L1_gnn_W_self, L1_gnn_b_self), axis=-1)
    x = _layernorm(x + _L2_gnn_ref(x, edge_index, edge_attr_128, L2_gnn_question_emb), axis=-1)
    x = _layernorm(x + _L3_gnn_ref(x, edge_index, edge_type_9, 3125, L3_gnn_W_msg, L3_gnn_b_msg, L3_gnn_edge_embed, L3_gnn_W_ih, L3_gnn_W_hh, L3_gnn_b_ih, L3_gnn_b_hh), axis=-1)
    return x

_drawn_inputs = setup_inputs


def setup_inputs(seed=0):
    import zlib

    import numpy as np

    out = dict(_drawn_inputs(seed))
    spreads = {}
    factors = {'edge_attr_128': 6.95,
     'L2_gnn_question_emb': 6.9,
     'L3_gnn_b_ih': 6.657,
     'L3_gnn_b_hh': 8.0}
    for name, (base, spread) in spreads.items():
        noise = np.random.default_rng([zlib.crc32(name.encode()), seed]).standard_normal(out[name].shape)
        drawn = base * np.exp(spread * noise) if base else spread * noise
        out[name] = jnp.asarray(drawn.astype(out[name].dtype))
    for name, factor in factors.items():
        out[name] = (out[name] * factor).astype(out[name].dtype)
    return out
```

```python
from contextlib import ExitStack

import concourse.bass as bass
from concourse import mybir

ALU = mybir.AluOpType
ACT = mybir.ActivationFunctionType
F32 = mybir.dt.float32
BF16 = mybir.dt.bfloat16
I32 = mybir.dt.int32
AXX = mybir.AxisListType.X

D = 128
N = 3125
E = 53125
B = 125
NB = N // B
G = 5
GB = NB // G
GW = GB * B
HALF = (313, 312)
T = E // B
CT = 25
NCH = T // CT
PIECE = GB * GW
ROW = 3136
NPIECE = G * G
ELEMS = NPIECE * 128 * ROW
F = 12
FN = F + 1
EPS = 1e-5
MAGIC = 12582912.0
FAR = 16777216.0


class Steps:

    def __init__(self, eng, sem):
        self.eng, self.sem, self.n = eng, sem, 0

    def __call__(self, ins):
        self.n += 1
        ins.then_inc(self.sem, 1)
        self.eng.wait_ge(self.sem, self.n)


def program(nc, x, src, dst, attr, ty2, ty9, mem, wih0, bih0, bhh0, wt, wtb, linb,
            wd, bd, wc, bc, ws, bs, quest, wmsg, bmsg, embed, wih, whh, bih, bhh, out):
    with ExitStack() as ctx:
        def sb(name, shape, dt=F32):
            return ctx.enter_context(nc.sbuf_tensor(name, shape, dt))

        def pb(name):
            return ctx.enter_context(nc.psum_tensor(name, [128, 512], F32))

        def sem(name):
            return ctx.enter_context(nc.semaphore(name))

        dense = [nc.dram_tensor(n, [ELEMS, 1], F32, kind="Internal").ap() for n in ("count_all", "count_ctrl", "sim_sum")]
        dense_v = [a.rearrange("(q p n) o -> q p (n o)", p=128, n=ROW) for a in dense]
        COUNT, CTRL, SIM = 0, 1, 2

        ring = sb("ring", [128, G, 3200])
        xa = sb("xa", [B, NB, D])
        xb = sb("xb", [B, NB, D])
        xc = sb("xc", [B, NB, D])
        xT = sb("xT", [D, N])
        cT = sb("cT", [D, N])
        wtr = sb("wtr", [128, 2, 1024])
        ei = xb[:, :, :].rearrange("p b d -> p (b d)").bitcast(I32)[:, 0:4 * T].rearrange("p (n t) -> p n t", t=T)
        ef = [cT[0:B, n * T:(n + 1) * T] for n in range(7)] + \
             [xc[:, :, :].rearrange("p b d -> p (b d)")[:, n * T:(n + 1) * T] for n in range(5)]
        feats = sb("feats", [B, T, F], BF16)
        vals = sb("vals", [B, T, 3])
        norm2 = sb("norm2", [B, T])
        dots = sb("dots", [B, T])
        iot_i = sb("iot_i", [128, 129], I32)
        iot = sb("iot", [128, 129])
        ident = sb("ident", [128, 128])
        tri = sb("tri", [128, 128])
        iota_bf = sb("iota_bf", [128, 128], BF16)
        zrow = sb("zrow", [128, 512], BF16)
        q_bc = sb("q_bc", [B, D])
        q_n = sb("q_n", [B, D])
        q_s = sb("q_s", [B, 4])
        kb = sb("kb", [B, B])
        kcol = sb("kcol", [B, 1])
        v3 = sb("v3", [B, 3])
        s3 = sb("s3", [B, 3])
        same = sb("same", [B, B])
        same_tri = sb("same_tri", [B, B])
        rank = sb("rank", [B, 1])
        idx = sb("idx", [B, 1], I32)
        ohoff = sb("ohoff", [B, B], BF16)
        ohdb = sb("ohdb", [B, NB])
        rhs12 = sb("rhs12", [B, NB, F], BF16)
        counts = sb("counts", [B, NB, FN])
        countsT = sb("countsT", [FN, N])
        halfdeg = sb("halfdeg", [B, NB])
        r0 = sb("r0", [FN, D])
        r1 = sb("r1", [FN, D])
        r3 = sb("r3", [FN, D])
        mem_c = sb("mem_c", [D, 1])
        wih0_s = sb("wih0_s", [D, 3 * D])
        b0 = sb("b0", [D, 2, 3])
        gru = sb("gru", [D, 10])
        wtb_s = sb("wtb_s", [D, D])
        nwT = sb("nwT", [D, D])
        w1 = sb("w1", [D, 3, D])
        wmsg_s = sb("wmsg_s", [D, D])
        wih_s = sb("wih_s", [D, 3 * D])
        whh_s = sb("whh_s", [D, 3 * D])
        b3 = sb("b3", [D, 2, 3])
        b3s = sb("b3s", [D, 3])
        agg = sb("agg", [D, GW])
        hT = sb("hT", [D, GW])
        mT = sb("mT", [D, GW])
        gr = sb("gr", [D, 4, GW])
        y = sb("y", [B, GB, D])
        yc = sb("yc", [B, GB, D])
        sq = sb("sq", [B, GB, D])
        st = sb("st", [B, 4, GB])
        epsc = sb("epsc", [128, 1])
        mark = sb("mark", [1, 1])

        acc = [pb("acc0"), pb("acc1")]
        dn = [pb("dn0"), pb("dn1")]
        tp = [pb("tp0"), pb("tp1")]
        cnt = pb("cnt")
        gx = pb("gx")

        names = """ld_edges ld_x ld_w ld_q zeroed iota_done consts edges_ready attr_in0 attr_in1 prod_done square_done
            sums_done vals_ready tile_ready keyrow same_ready tile_sums idx_ready tile_done scat0 scat1 scat2
            cnt_init counts_psum counts_sb countsT_ps countsT_sb q_ssq q_norm q_ready norm_in norm_out
            gi gru_ready0 gru_rz gru_t gru_n u_ready wt_in0 wt_in1 wt_used nw_psum nw_ready w_small
            acc_ready acc_free h_ready lin_ready lin_free xc_ready sq_ready sd_in sd_ready x_ready
            t_ready t_free xT_ready c0_ready tr_ready tr_free msg_ready m_ready gates_ready rz_ready gx_free n_in n_ready
            yT_ready yt_ready y_ready out_done zero_done dense_ready piece_used dve act pool agg_used x2_ready""".split()
        S = {n: sem(n) for n in names}
        piece_in = [sem(f"piece_in{k}") for k in range(G)]

        attr_v = attr.rearrange("(p t) d -> p t d", p=B)
        attr_buf = [ring[0:B, 0, :].rearrange("p (t d) -> p t d", d=D), ring[0:B, 1, :].rearrange("p (t d) -> p t d", d=D)]
        prod = ring[0:B, 2, :].rearrange("p (t d) -> p t d", d=D)
        squa = ring[0:B, 3, :].rearrange("p (t d) -> p t d", d=D)
        zero = ring[:, 4, 0:ROW]
        PASSES = [(COUNT, xa), (COUNT, xb), (CTRL, xb), (SIM, xc), (SIM, xa), (COUNT, xb)]
        L0, L1A, L1B, L2A, L2B, L3 = range(6)

        block = ctx.enter_context(nc.Block())

        @block.sync
        def _(sp):
            for n, a in enumerate((dst, src, ty2, ty9)):
                sp.dma_start(ei[:, n, :], a.rearrange("(p t) -> p t", p=B)).then_inc(S["ld_edges"], 16)
            sp.dma_start(q_bc[:, :], quest.partition_broadcast(B).rearrange("p a d -> p (a d)")).then_inc(S["ld_q"], 16)
            sp.dma_start(xa[:, :, :], x.rearrange("(b p) d -> p b d", p=B)).then_inc(S["ld_x"], 16)
            for c in range(NCH):
                if c >= 2:
                    sp.wait_ge(S["prod_done"], c - 1)
                    sp.wait_ge(S["square_done"], c - 1)
                for lo, hi in ((0, 112), (112, B)):
                    sp.dma_start(attr_buf[c % 2][lo:hi], attr_v[lo:hi, c * CT:(c + 1) * CT, :]).then_inc(S[f"attr_in{c % 2}"], 16)
            sp.wait_ge(S["zeroed"], 1)
            for m in range(3):
                for q in range(NPIECE):
                    sp.dma_start(dense_v[m][q], zero).then_inc(S["zero_done"], 16)
            for m in range(3):
                sp.wait_ge(S[f"scat{m}"], 16 * T)
            for n, (m, _) in enumerate(PASSES):
                for g in range(G):
                    for k in range(G):
                        at = n * G + g
                        if at >= 1:
                            sp.wait_ge(S["piece_used"], (at - 1) * G + k + 1)
                        else:
                            sp.wait_ge(S["square_done"], NCH)
                            sp.wait_ge(S["prod_done"], NCH)
                            sp.wait_ge(S["sums_done"], NCH)
                        sp.dma_start(ring[:, k, 0:ROW], dense_v[m][g * G + k]).then_inc(piece_in[k], 16)
            out_v = out.rearrange("(b p) d -> p b d", p=B)
            for g in range(G):
                sp.wait_ge(S["x_ready"], 3 * G + g + 1)
                sp.dma_start(out_v[:, g * GB:(g + 1) * GB, :], xa[:, g * GB:(g + 1) * GB, :]).then_inc(S["out_done"], 16)
            sp.wait_ge(S["out_done"], 16 * G)

        @block.gpsimd
        def _(pool):
            nc.gpsimd.iota(iot_i[:, 0:128], pattern=[[1, 128]], base=0, channel_multiplier=0).then_inc(S["iota_done"], 1)
            nc.gpsimd.iota(iot_i[:, 128:129], pattern=[[1, 1]], base=0, channel_multiplier=1).then_inc(S["iota_done"], 1)
            nc.gpsimd.memset(zero, 0.0).then_inc(S["zeroed"], 1)
            pool.wait_ge(S["q_ready"], 1)
            for c in range(NCH):
                pool.wait_ge(S[f"attr_in{c % 2}"], 32 * (c // 2 + 1))
                if c >= 1:
                    pool.wait_ge(S["sums_done"], c)
                nc.gpsimd.tensor_tensor(prod, attr_buf[c % 2], q_n[:, :].unsqueeze(1).to_broadcast([B, CT, D]),
                                        ALU.mult).then_inc(S["prod_done"], 1)
            pool.wait_ge(S["zero_done"], 16 * 3 * NPIECE)
            nc.gpsimd.memset(mark[:, :], 0.0).then_inc(S["tile_done"], 1)
            last_elem = pool.to_reg(ELEMS - 1)
            with pool.Fori(0, T) as t:
                pool.wait_ge(S["idx_ready"], t + 1)
                nc.gpsimd.tensor_tensor(mark[:, :], kcol[0:1, :], kcol[0:1, :], ALU.add).then_inc(S["tile_done"], 1)
                for m in range(3):
                    nc.gpsimd.indirect_dma_start(
                        dense[m], bass.IndirectOffsetOnAxis(ap=idx[:, 0:1], axis=0), s3[:, m:m + 1], None,
                        bounds_check=last_elem, oob_is_err=True, compute_op=ALU.add).then_inc(S[f"scat{m}"], 16)

        @block.scalar
        def _(act):
            small = [(mem_c[:, :], mem), (wih0_s[:, :], wih0), (b0[:, 0, :], bih0), (b0[:, 1, :], bhh0), (wtb_s[:, :], wtb),
                     (w1[:, 0, :], wd), (w1[:, 1, :], wc), (w1[:, 2, :], ws), (wmsg_s[:, :], wmsg), (wih_s[:, :], wih),
                     (whh_s[:, :], whh), (b3[:, 0, :], bih), (b3[:, 1, :], bhh)]
            for o, i in small:
                act.dma_start(o, i).then_inc(S["ld_w"], 16)
            act.wait_ge(S["w_small"], 1)
            for o, i in ((r0[12:13, :], linb), (r1[0:1, :], bd), (r1[1:2, :], bc), (r1[12:13, :], bs), (r3[2:3, :], bmsg)):
                act.dma_start(o, i.rearrange("(a d) -> a d", a=1)).then_inc(S["ld_w"], 16)
            act.dma_start(r3[3:12, :], embed).then_inc(S["ld_w"], 16)
            act.wait_ge(S["q_ssq"], 1)
            nc.scalar.activation(q_s[:, 1:2], q_s[:, 0:1], ACT.Sqrt).then_inc(S["q_norm"], 1)
            act.wait_ge(S["gi"], 1)
            act.wait_ge(S["gru_ready0"], 1)
            for k in range(2):
                nc.scalar.activation(gru[:, k:k + 1], dn[0][:, k:k + 1], ACT.Sigmoid, bias=gru[:, 6 + k:7 + k]).then_inc(S["gru_rz"], 1)
            act.wait_ge(S["gru_t"], 1)
            nc.scalar.activation(gru[:, 4:5], gru[:, 3:4], ACT.Tanh).then_inc(S["gru_n"], 1)
            for c in range(16):
                if c >= 2:
                    act.wait_ge(S["wt_used"], c - 1)
                act.dma_start(wtr[:, c % 2, :], wt[:, c * 1024:(c + 1) * 1024]).then_inc(S[f"wt_in{c % 2}"], 16)
            for c in range(NCH):
                act.wait_ge(S[f"attr_in{c % 2}"], 32 * (c // 2 + 1))
                if c >= 1:
                    act.wait_ge(S["sums_done"], c)
                nc.scalar.activation(squa, attr_buf[c % 2], ACT.Square).then_inc(S["square_done"], 1)
            act.wait_ge(S["norm_in"], 1)
            nc.scalar.activation(norm2[:, :], norm2[:, :], ACT.Sqrt).then_inc(S["norm_out"], 1)
            for b in range(NB):
                act.wait_ge(S["countsT_ps"], b + 1)
                nc.scalar.copy(countsT[:, b * B:(b + 1) * B], tp[b % 2][0:FN, 0:B]).then_inc(S["countsT_sb"], 1)

            def transposed(turn):
                for c in range(7):
                    act.wait_ge(S["t_ready"], turn * 7 + c + 1)
                    lo, hi = c * 4, min(NB, c * 4 + 4)
                    nc.scalar.copy(xT[:, lo * B:hi * B], tp[c % 2][:, 0:(hi - lo) * B]).then_inc(S["t_free"], 1)

            def group_out(n, g, to):
                act.wait_ge(S["piece_used"], G * (n * G + g + 1))
                if n in (L0, L1B, L2A, L2B, L3) and n * G + g > 0 and not (n == L1B and g == 0):
                    act.wait_ge(S["agg_used"], used(n, g))
                for h in range(2):
                    nc.scalar.copy(to[:, h * HALF[0]:h * HALF[0] + HALF[h]], acc[h][:, 0:HALF[h]]).then_inc(S["acc_free"], 1)

            def used(n, g):
                return {L0: 0, L1B: G, L2A: 2 * G, L2B: 3 * G, L3: 4 * G}[n] + g

            def norm_part(k):
                act.wait_ge(S["xc_ready"], k + 1)
                nc.scalar.activation(sq[:, :, :], yc[:, :, :], ACT.Square).then_inc(S["sq_ready"], 1)
                act.wait_ge(S["sd_in"], k + 1)
                nc.scalar.activation(st[:, 2, :], st[:, 1, :], ACT.Sqrt, bias=epsc[0:B, 0:1], scale=1.0 / D).then_inc(S["sd_ready"], 1)

            transposed(0)
            for g in range(G):
                group_out(L0, g, agg)
                norm_part(g)
            transposed(1)
            for g in range(G):
                group_out(L1A, g, cT[:, g * GW:(g + 1) * GW])
            for g in range(G):
                group_out(L1B, g, agg)
                norm_part(G + g)
            for g in range(G):
                group_out(L2A, g, agg)
            for g in range(G):
                group_out(L2B, g, agg)
                norm_part(2 * G + g)
            transposed(2)
            for g in range(G):
                group_out(L3, g, agg)
                for h in range(2):
                    w, lo = HALF[h], h * HALF[0]
                    act.wait_ge(S["msg_ready"], 2 * g + h + 1)
                    nc.scalar.copy(mT[:, lo:lo + w], dn[h][:, 0:w]).then_inc(S["m_ready"], 1)
                    act.wait_ge(S["gates_ready"], 2 * g + h + 1)
                    for k in range(2):
                        nc.scalar.activation(gr[:, k, lo:lo + w], tp[k][:, 0:w], ACT.Sigmoid, bias=b3s[:, k:k + 1]).then_inc(S["rz_ready"], 1)
                    act.wait_ge(S["n_in"], 2 * g + h + 1)
                    nc.scalar.activation(gr[:, 2, lo:lo + w], gr[:, 3, lo:lo + w], ACT.Tanh, bias=b3[:, 0, 2:3]).then_inc(S["n_ready"], 1)
                act.wait_ge(S["yt_ready"], g + 1)
                nc.scalar.copy(y[:, 0:4, :], dn[0][0:B, :].rearrange("p (b d) -> p b d", d=D)).then_inc(S["y_ready"], 1)
                nc.scalar.copy(y[:, 4, :], dn[1][0:B, 0:D]).then_inc(S["y_ready"], 1)
                norm_part(3 * G + g)

        @block.tensor
        def _(pe):
            pe.wait_ge(S["ld_w"], 16 * 19)
            for k in range(3):
                last = nc.tensor.matmul(dn[0][:, k:k + 1], wih0_s[:, k * D:(k + 1) * D], mem_c[:, :], start=True, stop=True)
            last.then_inc(S["gi"], 1)
            pe.wait_ge(S["u_ready"], 1)
            for c in range(16):
                pe.wait_ge(S[f"wt_in{c % 2}"], 16 * (c // 2 + 1))
                for o in range(8):
                    last = nc.tensor.matmul(dn[1][:, c * 8 + o:c * 8 + o + 1], wtr[:, c % 2, o * D:(o + 1) * D], gru[:, 5:6],
                                            start=True, stop=True)
                last.then_inc(S["wt_used"], 1)
            pe.wait_ge(S["consts"], 1)
            nc.tensor.matmul(cnt[0:B, 0:NB * F], zrow[0:B, 0:B], zrow[0:B, 0:NB * F], start=True, stop=False,
                             skip_group_check=True).then_inc(S["cnt_init"], 1)
            pe.wait_ge(S["cnt_init"], 1)
            with pe.Fori(0, T) as t:
                pe.wait_ge(S["tile_ready"], t + 1)
                nc.tensor.transpose(tp[0][0:B, 0:B], kb[:, :], ident[0:B, 0:B]).then_inc(S["keyrow"], 1)
                nc.tensor.matmul(cnt[0:B, 0:NB * F], ohoff[:, :], rhs12[:, :, :].rearrange("p b f -> p (b f)"),
                                 start=False, stop=False, skip_group_check=True)
                pe.wait_ge(S["same_ready"], t + 1)
                nc.tensor.matmul(tp[1][0:B, 0:3], same[:, :], v3[:, :], start=True, stop=True).then_inc(S["tile_sums"], 1)
            nc.tensor.matmul(cnt[0:B, 0:NB * F], zrow[0:B, 0:B], zrow[0:B, 0:NB * F], start=False, stop=True,
                             skip_group_check=True).then_inc(S["counts_psum"], 1)
            pe.wait_ge(S["counts_sb"], 1)
            for b in range(NB):
                if b >= 2:
                    pe.wait_ge(S["countsT_sb"], b - 1)
                nc.tensor.transpose(tp[b % 2][0:FN, 0:B], counts[:, b, :], ident[0:B, 0:B]).then_inc(S["countsT_ps"], 1)
            pe.wait_ge(S["countsT_sb"], NB)

            def transposes(turn, xs):
                for c in range(7):
                    if turn * 7 + c >= 2:
                        pe.wait_ge(S["t_free"], turn * 7 + c - 1)
                    for b in range(c * 4, min(NB, c * 4 + 4)):
                        last = nc.tensor.transpose(tp[c % 2][:, (b % 4) * B:(b % 4 + 1) * B], xs[:, b, :], ident[0:B, 0:B])
                    last.then_inc(S["t_ready"], 1)

            def aggregate(n, g):
                xs = PASSES[n][1]
                if n * G + g >= 1:
                    pe.wait_ge(S["acc_free"], 2 * (n * G + g))
                for k in range(G):
                    pe.wait_ge(piece_in[k], 16 * (n * G + g + 1))
                    for r in range(GB):
                        s = k * GB + r
                        for h in range(2):
                            lo = r * GW + h * HALF[0]
                            last = nc.tensor.matmul(acc[h][:, 0:HALF[h]], xs[:, s, :], ring[0:B, k, lo:lo + HALF[h]],
                                                    start=(s == 0), stop=(s == NB - 1))
                    last.then_inc(S["piece_used"], 1)

            def linear(k, g, terms, bias):
                pe.wait_ge(S["h_ready"], k * G + g + 1)
                if k * G + g >= 1:
                    pe.wait_ge(S["lin_free"], k * G + g)
                for b in range(GB):
                    o = dn[b // 4][0:B, (b % 4) * D:(b % 4 + 1) * D]
                    for i, (lhs, base, w) in enumerate(terms):
                        nc.tensor.matmul(o, lhs[:, (base + b) * B:(base + b + 1) * B], w, start=(i == 0), stop=False)
                    last = nc.tensor.matmul(o, countsT[:, (g * GB + b) * B:(g * GB + b + 1) * B], bias, start=False, stop=True)
                last.then_inc(S["lin_ready"], 1)

            pe.wait_ge(S["ld_x"], 16)
            transposes(0, xa)
            pe.wait_ge(S["nw_ready"], 1)
            for g in range(G):
                aggregate(L0, g)
                linear(0, g, [(hT, 0, nwT[:, :])], r0[:, :])
            pe.wait_ge(S["x_ready"], G)
            transposes(1, xb)
            for g in range(G):
                aggregate(L1A, g)
            for g in range(G):
                aggregate(L1B, g)
                linear(1, g, [(hT, 0, w1[:, 0, :]), (agg, 0, w1[:, 1, :]), (xT, g * GB, w1[:, 2, :])], r1[:, :])
            pe.wait_ge(S["x_ready"], 2 * G)
            for n in (L2A, L2B):
                if n == L2B:
                    pe.wait_ge(S["x2_ready"], G)
                for g in range(G):
                    aggregate(n, g)
                    pe.wait_ge(S["acc_free"], 2 * (n * G + g + 1))
                    if g or n == L2B:
                        pe.wait_ge(S["tr_free"], (n - L2A) * G + g)
                    for b in range(GB):
                        last = nc.tensor.transpose(dn[b // 4][0:B, (b % 4) * D:(b % 4 + 1) * D], agg[:, b * B:(b + 1) * B], ident[:, :])
                    last.then_inc(S["tr_ready"], 1)
            pe.wait_ge(S["x_ready"], 3 * G)
            transposes(2, xb)
            for g in range(G):
                aggregate(L3, g)
                pe.wait_ge(S["acc_free"], 2 * (L3 * G + g + 1))
                if g:
                    pe.wait_ge(S["y_ready"], 2 * g)
                for h in range(2):
                    w, lo = HALF[h], h * HALF[0]
                    nc.tensor.matmul(dn[h][:, 0:w], wmsg_s[:, :], agg[:, lo:lo + w], start=True, stop=False)
                    nc.tensor.matmul(dn[h][:, 0:w], r3[:, :], countsT[:, g * GW + lo:g * GW + lo + w],
                                     start=False, stop=True).then_inc(S["msg_ready"], 1)
                for h in range(2):
                    w, lo = HALF[h], h * HALF[0]
                    m, hh = mT[:, lo:lo + w], xT[:, g * GW + lo:g * GW + lo + w]
                    pe.wait_ge(S["m_ready"], 2 * g + h + 1)
                    if g or h:
                        pe.wait_ge(S["rz_ready"], 2 * (2 * g + h))
                        pe.wait_ge(S["n_in"], 2 * g + h)
                    else:
                        pe.wait_ge(S["t_free"], 21)
                    for k in range(2):
                        nc.tensor.matmul(tp[k][:, 0:w], wih_s[:, k * D:(k + 1) * D], m, start=True, stop=False)
                        nc.tensor.matmul(tp[k][:, 0:w], whh_s[:, k * D:(k + 1) * D], hh, start=False, stop=True)
                    nc.tensor.matmul(gx[:, 0:w], wih_s[:, 2 * D:3 * D], m, start=True, stop=True)
                    nc.tensor.matmul(cnt[:, 0:w], whh_s[:, 2 * D:3 * D], hh, start=True, stop=True).then_inc(S["gates_ready"], 1)
                pe.wait_ge(S["yT_ready"], 2 * (g + 1))
                for b in range(GB):
                    last = nc.tensor.transpose(dn[b // 4][0:B, (b % 4) * D:(b % 4 + 1) * D], hT[:, b * B:(b + 1) * B], ident[:, :])
                last.then_inc(S["yt_ready"], 1)

        @block.vector
        def _(dve):
            v = nc.vector
            step = Steps(dve, S["dve"])
            step(v.memset(r0[:, :], 0.0))
            step(v.memset(r1[:, :], 0.0))
            step(v.memset(epsc[:, :], EPS))
            v.memset(r3[:, :], 0.0).then_inc(S["w_small"], 1)
            step(v.memset(zrow[:, :], 0.0))
            dve.wait_ge(S["iota_done"], 2)
            step(v.tensor_copy(iot[:, :], iot_i[:, :]))
            step(v.tensor_copy(iota_bf[:, :], iot_i[:, 0:128]))
            step(v.tensor_scalar(ident[:, :], iot[:, 0:128], iot[:, 128:129], None, ALU.is_equal))
            step(v.memset(counts[:, :, :], 1.0))
            v.tensor_scalar(tri[:, :], iot[:, 0:128], iot[:, 128:129], None, ALU.is_lt).then_inc(S["consts"], 1)
            dve.wait_ge(S["ld_q"], 16)
            step(v.tensor_tensor(q_n[:, :], q_bc[:, :], q_bc[:, :], ALU.mult))
            step(v.tensor_reduce(q_s[:, 2:3], q_n[:, :], AXX, ALU.add))
            v.tensor_scalar(q_s[:, 0:1], q_s[:, 2:3], 1e-24, None, ALU.max).then_inc(S["q_ssq"], 1)
            dve.wait_ge(S["q_norm"], 1)
            step(v.reciprocal(q_s[:, 3:4], q_s[:, 1:2]))
            v.tensor_scalar(q_n[:, :], q_bc[:, :], q_s[:, 3:4], None, ALU.mult).then_inc(S["q_ready"], 1)
            dve.wait_ge(S["ld_w"], 16 * 19)
            step(v.tensor_tensor(b3s[:, :], b3[:, 0, :], b3[:, 1, :], ALU.add))
            v.tensor_tensor(gru[:, 6:8], b0[:, 0, 0:2], b0[:, 1, 0:2], ALU.add).then_inc(S["gru_ready0"], 1)
            dve.wait_ge(S["gru_rz"], 2)
            step(v.tensor_tensor(gru[:, 2:3], gru[:, 0:1], b0[:, 1, 2:3], ALU.mult))
            step(v.tensor_tensor(gru[:, 2:3], gru[:, 2:3], b0[:, 0, 2:3], ALU.add))
            v.tensor_tensor(gru[:, 3:4], gru[:, 2:3], dn[0][:, 2:3], ALU.add).then_inc(S["gru_t"], 1)
            step(v.tensor_scalar(gru[:, 8:9], gru[:, 1:2], -1.0, 1.0, ALU.mult, ALU.add))
            dve.wait_ge(S["gru_n"], 1)
            v.tensor_tensor(gru[:, 5:6], gru[:, 8:9], gru[:, 4:5], ALU.mult).then_inc(S["u_ready"], 1)
            dve.wait_ge(S["ld_edges"], 64)
            dstf, srcf, t2, t9, db, sbl, dg, sk, do, so, key, tmp = (ef[n] for n in range(12))
            for n in range(4):
                step(v.tensor_copy(ef[n], ei[:, n, :]))

            def floor_div(o, i, by):
                step(v.tensor_scalar(tmp, i, 1.0 / by, -0.5 + 0.5 / by, ALU.mult, ALU.add))
                step(v.tensor_scalar(o, tmp, MAGIC, -MAGIC, ALU.add, ALU.add))

            floor_div(db, dstf, B)
            floor_div(sbl, srcf, B)
            floor_div(dg, dstf, GW)
            floor_div(sk, sbl, GB)
            step(v.scalar_tensor_tensor(do, db, -float(B), dstf, ALU.mult, ALU.add))
            step(v.scalar_tensor_tensor(so, sbl, -float(B), srcf, ALU.mult, ALU.add))
            step(v.scalar_tensor_tensor(key, dg, float(G), sk, ALU.mult, ALU.add))
            step(v.scalar_tensor_tensor(key, key, 128.0, so, ALU.mult, ALU.add))
            step(v.scalar_tensor_tensor(key, key, float(ROW), dstf, ALU.mult, ALU.add))
            step(v.scalar_tensor_tensor(key, dg, -float(GW), key, ALU.mult, ALU.add))
            step(v.scalar_tensor_tensor(tmp, sk, -float(GB), sbl, ALU.mult, ALU.add))
            step(v.scalar_tensor_tensor(key, tmp, float(GW), key, ALU.mult, ALU.add))
            step(v.tensor_scalar(feats[:, :, 0], t2, 0.0, None, ALU.is_equal))
            step(v.tensor_scalar(feats[:, :, 1], t2, 0.0, None, ALU.not_equal))
            step(v.memset(feats[:, :, 2], 1.0))
            step(v.tensor_scalar(tmp, t9, 0.0, 8.0, ALU.max, ALU.min))
            step(v.tensor_tensor(feats[:, :, 3:12], tmp.unsqueeze(2).to_broadcast([B, T, 9]),
                                 iot[0:B, 0:9].unsqueeze(1).to_broadcast([B, T, 9]), ALU.is_equal))
            step(v.memset(vals[:, :, 0], 1.0))
            step(v.tensor_scalar(vals[:, :, 1], t2, 0.0, None, ALU.not_equal))
            for c in range(NCH):
                dve.wait_ge(S["square_done"], c + 1)
                step(v.tensor_reduce(norm2[:, c * CT:(c + 1) * CT], squa, AXX, ALU.add))
                dve.wait_ge(S["prod_done"], c + 1)
                v.tensor_reduce(dots[:, c * CT:(c + 1) * CT], prod, AXX, ALU.add).then_inc(S["sums_done"], 1)
            dve.wait_ge(S["sums_done"], NCH)
            v.tensor_scalar(norm2[:, :], norm2[:, :], 1e-24, None, ALU.max).then_inc(S["norm_in"], 1)
            dve.wait_ge(S["norm_out"], 1)
            step(v.reciprocal(norm2[:, :], norm2[:, :]))
            step(v.tensor_tensor(vals[:, :, 2], dots[:, :], norm2[:, :], ALU.mult))
            dve.wait_ge(S["wt_used"], 16)
            v.tensor_tensor(nwT[:, :], dn[1][:, 0:D], wtb_s[:, :], ALU.add).then_inc(S["nw_ready"], 1)
            base = step.n
            dve.wait_ge(S["tile_done"], 1)
            with dve.Fori(0, T) as t:
                def lk(k, ins):
                    ins.then_inc(S["dve"], 1)
                    dve.wait_ge(S["dve"], base + 4 * t + k)
                v.tensor_copy(kcol[:, :], key[:, bass.ds(t, 1)])
                v.tensor_copy(v3[:, :], vals[:, bass.ds(t, 1), :].rearrange("p a b -> p (a b)"))
                v.tensor_scalar(ohoff[:, :], iota_bf[0:B, 0:B], do[:, bass.ds(t, 1)], None, ALU.is_equal)
                lk(1, v.tensor_scalar(ohdb[:, :], iot[0:B, 0:NB], db[:, bass.ds(t, 1)], None, ALU.is_equal))
                v.tensor_tensor(rhs12[:, :, :], ohdb[:, :].unsqueeze(2).to_broadcast([B, NB, F]),
                                feats[:, bass.ds(t, 1), :].to_broadcast([B, NB, F]), ALU.mult)
                v.tensor_copy(kb[:, :], key[:, bass.ds(t, 1)].to_broadcast([B, B])).then_inc(S["tile_ready"], 1)
                dve.wait_ge(S["keyrow"], t + 1)
                lk(2, v.tensor_scalar(same[:, :], tp[0][0:B, 0:B], kcol[:, :], None, ALU.is_equal))
                v.tensor_tensor(same_tri[:, :], same[:, :], tri[0:B, 0:B], ALU.mult).then_inc(S["same_ready"], 1)
                dve.wait_ge(S["same_ready"], t + 1)
                lk(3, v.tensor_reduce(rank[:, :], same_tri[:, :], AXX, ALU.add))
                lk(4, v.scalar_tensor_tensor(idx[:, :], rank[:, :], FAR, kcol[:, :], ALU.mult, ALU.add))
                dve.wait_ge(S["tile_sums"], t + 1)
                v.tensor_copy(s3[:, :], tp[1][0:B, 0:3]).then_inc(S["idx_ready"], 1)
                dve.wait_ge(S["tile_done"], t + 2)
                for m in range(3):
                    dve.wait_ge(S[f"scat{m}"], 16 * (t + 1))
            step.n = base + 4 * T
            dve.wait_ge(S["counts_psum"], 1)
            v.tensor_copy(counts[:, :, 0:F], cnt[0:B, 0:NB * F].rearrange("p (b f) -> p b f", f=F)).then_inc(S["counts_sb"], 1)
            dve.wait_ge(S["counts_sb"], 1)
            step(v.tensor_scalar(halfdeg[:, :], counts[:, :, 2], 1.0, None, ALU.max))
            step(v.reciprocal(halfdeg[:, :], halfdeg[:, :]))
            step(v.tensor_scalar(halfdeg[:, :], halfdeg[:, :], 0.5, None, ALU.mult))

            def layernorm(k, g, xo):
                step(v.tensor_reduce(st[:, 0, :], y[:, :, :], AXX, ALU.add))
                step(v.tensor_scalar(st[:, 0, :], st[:, 0, :], 1.0 / D, None, ALU.mult))
                v.tensor_tensor(yc[:, :, :], y[:, :, :], st[:, 0, :].unsqueeze(2).to_broadcast([B, GB, D]), ALU.subtract)\
                    .then_inc(S["xc_ready"], 1)
                dve.wait_ge(S["sq_ready"], k * G + g + 1)
                v.tensor_reduce(st[:, 1, :], sq[:, :, :], AXX, ALU.add).then_inc(S["sd_in"], 1)
                dve.wait_ge(S["sd_ready"], k * G + g + 1)
                step(v.reciprocal(st[:, 3, :], st[:, 2, :]))
                v.tensor_tensor(xo[:, g * GB:(g + 1) * GB, :], yc[:, :, :], st[:, 3, :].unsqueeze(2).to_broadcast([B, GB, D]),
                                ALU.mult).then_inc(S["x_ready"], 1)
                dve.wait_ge(S["x_ready"], k * G + g + 1)

            def relu_add(k, g, xs):
                dve.wait_ge(S["lin_ready"], k * G + g + 1)
                v.scalar_tensor_tensor(y[:, 0:4, :], dn[0][0:B, :].rearrange("p (b d) -> p b d", d=D), 0.0,
                                       xs[:, g * GB:g * GB + 4, :], ALU.max, ALU.add)
                v.scalar_tensor_tensor(y[:, 4, :], dn[1][0:B, 0:D], 0.0, xs[:, g * GB + 4, :], ALU.max, ALU.add)\
                    .then_inc(S["lin_free"], 1)
                dve.wait_ge(S["lin_free"], k * G + g + 1)

            for g in range(G):
                dve.wait_ge(S["acc_free"], 2 * (L0 * G + g + 1))
                dve.wait_ge(S["t_free"], 7)
                v.tensor_tensor(hT[:, :], agg[:, :], xT[:, g * GW:(g + 1) * GW], ALU.add).then_inc(S["h_ready"], 1)
                dve.wait_ge(S["h_ready"], g + 1)
                dve.sem_inc(S["agg_used"], 1)
                relu_add(0, g, xa)
                layernorm(0, g, xb)
            for g in range(G):
                dve.wait_ge(S["acc_free"], 2 * (L1B * G + g + 1))
                dve.wait_ge(S["t_free"], 14)
                v.tensor_tensor(hT[:, :], cT[:, g * GW:(g + 1) * GW], agg[:, :], ALU.subtract).then_inc(S["h_ready"], 1)
                relu_add(1, g, xb)
                dve.sem_inc(S["agg_used"], 1)
                layernorm(1, g, xc)

            def mix(n, g, xs, to):
                dve.wait_ge(S["tr_ready"], (n - L2A) * G + g + 1)
                hd = halfdeg[:, g * GB:(g + 1) * GB].unsqueeze(2)
                v.tensor_tensor(yc[:, 0:4, :], dn[0][0:B, :].rearrange("p (b d) -> p b d", d=D),
                                hd[:, 0:4, :].to_broadcast([B, 4, D]), ALU.mult)
                v.tensor_tensor(yc[:, 4:5, :], dn[1][0:B, 0:D].unsqueeze(1), hd[:, 4:5, :].to_broadcast([B, 1, D]), ALU.mult)\
                    .then_inc(S["tr_free"], 1)
                dve.wait_ge(S["tr_free"], (n - L2A) * G + g + 1)
                dve.sem_inc(S["agg_used"], 1)
                step(v.scalar_tensor_tensor(to, xs[:, g * GB:(g + 1) * GB, :], 0.5, yc[:, :, :], ALU.mult, ALU.add))

            for g in range(G):
                mix(L2A, g, xc, xa[:, g * GB:(g + 1) * GB, :])
                dve.sem_inc(S["x2_ready"], 1)
            for g in range(G):
                mix(L2B, g, xa, y[:, :, :])
                step(v.tensor_tensor(y[:, :, :], y[:, :, :], xc[:, g * GB:(g + 1) * GB, :], ALU.add))
                layernorm(2, g, xb)
            for g in range(G):
                for h in range(2):
                    w, lo = HALF[h], h * HALF[0]
                    r, z, n_, t_ = (gr[:, k, lo:lo + w] for k in range(4))
                    xx = xT[:, g * GW + lo:g * GW + lo + w]
                    yy = hT[:, lo:lo + w]
                    dve.wait_ge(S["gates_ready"], 2 * g + h + 1)
                    dve.wait_ge(S["rz_ready"], 2 * (2 * g + h + 1))
                    step(v.scalar_tensor_tensor(t_, cnt[:, 0:w], b3[:, 1, 2:3], r, ALU.add, ALU.mult))
                    v.tensor_tensor(t_, t_, gx[:, 0:w], ALU.add).then_inc(S["n_in"], 1)
                    dve.wait_ge(S["n_ready"], 2 * g + h + 1)
                    if g and not h:
                        dve.wait_ge(S["yt_ready"], g)
                    step(v.tensor_tensor(yy, xx, n_, ALU.subtract))
                    step(v.tensor_tensor(yy, yy, z, ALU.mult))
                    step(v.tensor_tensor(yy, yy, n_, ALU.add))
                    v.tensor_tensor(yy, yy, xx, ALU.add).then_inc(S["yT_ready"], 1)
                dve.wait_ge(S["msg_ready"], 2 * (g + 1))
                dve.sem_inc(S["agg_used"], 1)
                dve.wait_ge(S["y_ready"], 2 * (g + 1))
                layernorm(3, g, xa)


_INS = ['x', 'src', 'dst', 'edge_attr_128', 'edge_type_2', 'edge_type_9', 'L0_gnn_memory', 'L0_gnn_gru_w_ih',
        'L0_gnn_gru_b_ih', 'L0_gnn_gru_b_hh', 'L0_gnn_wt_w', 'L0_gnn_wt_b', 'L0_gnn_lin_b', 'L1_gnn_W_data',
        'L1_gnn_b_data', 'L1_gnn_W_control', 'L1_gnn_b_control', 'L1_gnn_W_self', 'L1_gnn_b_self',
        'L2_gnn_question_emb', 'L3_gnn_W_msg', 'L3_gnn_b_msg', 'L3_gnn_edge_embed', 'L3_gnn_W_ih', 'L3_gnn_W_hh',
        'L3_gnn_b_ih', 'L3_gnn_b_hh']


def kernel(**inputs):
    import numpy as _np
    import concourse.bacc as _bacc
    from concourse import mybir as _mybir
    from concourse.bass_utils import run_bass_kernel_spmd as _run

    def lay(name, a):
        if name == 'L0_gnn_wt_b':
            return a.reshape(D, D).T
        if 'gru_b' in name or name in ('L3_gnn_b_ih', 'L3_gnn_b_hh'):
            return a.reshape(3, D).T
        if '_W_' in name or '_w_ih' in name or name in ('L0_gnn_memory', 'L0_gnn_wt_w'):
            return a.T
        return a

    nc = _bacc.Bacc("TRN2", target_bir_lowering=False, num_devices=1)
    arrays, args = {}, []
    for name in _INS:
        a = _np.ascontiguousarray(lay(name, _np.asarray(inputs[name])))
        arrays[f"in_{name}"] = a
        args.append(nc.dram_tensor(f"in_{name}", a.shape, _mybir.dt.from_np(a.dtype), kind="ExternalInput").ap())
    args.append(nc.dram_tensor("out_0", (N, D), _mybir.dt.float32, kind="ExternalOutput").ap())
    program(nc, *args)
    r = _run(nc, [arrays], core_ids=[0])
    return r.results[0]["out_0"]
```

```python
from contextlib import ExitStack

import concourse.bass as bass
from concourse import mybir

ALU = mybir.AluOpType
ACT = mybir.ActivationFunctionType
F32 = mybir.dt.float32
BF16 = mybir.dt.bfloat16
I32 = mybir.dt.int32
AXX = mybir.AxisListType.X

D = 128
N = 3125
E = 53125
B = 125
NB = N // B
G = 5
GB = NB // G
GW = GB * B
HALF = (313, 312)
T = E // B
CT = 25
NCH = T // CT
PIECE = GB * GW
ROW = 3136
NPIECE = G * G
W3 = 3
WIN = [(25 * c + 13) // 17 for c in range(NCH)]
KEYS = W3 * NB
SLOTS = NB * NB + NB
LANES = 128
KC = 4
RING = 4
OHR = 5
CAP_CUT = 0
ELEMS = NPIECE * 128 * ROW
F = 12
FN = F + 1
EPS = 1e-5
MAGIC = 12582912.0
FAR = 16777216.0


class Steps:

    def __init__(self, eng, sem):
        self.eng, self.sem, self.n = eng, sem, 0

    def __call__(self, ins):
        self.n += 1
        ins.then_inc(self.sem, 1)
        self.eng.wait_ge(self.sem, self.n)


def program(nc, x, src, dst, attr, ty2, ty9, mem, wih0, bih0, bhh0, wt, wtb, linb,
            wd, bd, wc, bc, ws, bs, quest, wmsg, bmsg, embed, wih, whh, bih, bhh, out):
    with ExitStack() as ctx:
        def sb(name, shape, dt=F32):
            return ctx.enter_context(nc.sbuf_tensor(name, shape, dt))

        def pb(name):
            return ctx.enter_context(nc.psum_tensor(name, [128, 512], F32))

        def sem(name):
            return ctx.enter_context(nc.semaphore(name))

        COUNT, CTRL, SIM = 0, 1, 2
        dts = [BF16, BF16, F32]
        dense = [nc.dram_tensor(n, [ELEMS + 128, 1], dt, kind="Internal").ap()
                 for n, dt in zip(("count_all", "count_ctrl", "sim_sum"), dts)]
        over = [nc.dram_tensor(n, [ELEMS + 128, 1], F32, kind="Internal").ap() for n in ("over_all", "over_ctrl")]
        def pieces(a):
            return a[0:ELEMS, :].rearrange("(q p n) o -> q p (n o)", p=128, n=ROW)
        dense_v = [pieces(a) for a in dense]
        over_v = [pieces(a) for a in over]
        over_dst = [over[0], over[1], dense[SIM]]
        buckets = [nc.dram_tensor(f"bucket{k}", [LANES * SLOTS, 2], F32, kind="Internal").ap() for k in range(KC)]

        ring = sb("ring", [128, RING, 3200])
        xa = sb("xa", [128, NB, D])
        xb = sb("xb", [128, NB, D])
        xc = sb("xc", [128, NB, D])
        xT = sb("xT", [D, N])
        cT = sb("cT", [D, N])
        wtr = xT[:, 0:2048].rearrange("p (a n) -> p a n", a=2)
        xs3 = [sb(f"xs3_{i}", [128, 3, NB, D], BF16) for i in range(2)]
        obuf = sb("obuf", [128, GW])
        work = sb("work", [128, GB * GW + 64])

        def part(at, shape, dt=F32, lanes=B):
            n = 1
            for d in shape:
                n *= d
            words = n if dt == F32 else (n + 1) // 2
            a = work[0:lanes, at:at + words]
            if dt != F32:
                a = a.bitcast(dt)[:, 0:n]
            if len(shape) == 2:
                a = a.rearrange("p (a b) -> p a b", b=shape[1])
            return a

        ei = xb[0:B, :, :].rearrange("p b d -> p (b d)").bitcast(I32)[:, 0:4 * T].rearrange("p (n t) -> p n t", t=T)
        xbf = xb[0:B, :, :].rearrange("p b d -> p (b d)")
        xcf = xc[0:B, :, :].rearrange("p b d -> p (b d)")
        ef = [cT[0:B, n * T:(n + 1) * T] for n in range(7)] + [xcf[:, n * T:(n + 1) * T] for n in range(7)]
        efx = [xbf[:, n * T:(n + 1) * T] for n in range(4, 7)]
        rec = sb("rec", [B, T, 2])
        simv = sb("simv", [B, T])
        slot = sb("slot", [B, T], I32)
        notok = sb("notok", [B, T])
        norm2 = sb("norm2", [B, 2, CT])
        normr = sb("normr", [B, 2, CT])
        dots = sb("dots", [B, 2, CT])
        iot_i = sb("iot_i", [128, 129], I32)
        iot = sb("iot", [128, 129])
        ident = sb("ident", [128, 128])
        tri = sb("tri", [128, 128])
        before = sb("before", [B, B], BF16)
        ones_bf = sb("ones_bf", [128, 128], BF16)
        iota_bf = sb("iota_bf", [128, 128], BF16)
        zrow = sb("zrow", [128, 512], BF16)
        q_bc = sb("q_bc", [B, D])
        q_n = sb("q_n", [B, D])
        q_s = sb("q_s", [B, 4])
        winoff = sb("winoff", [B, 3, NCH])
        oh = part(0, [CT, KEYS], BF16)
        lane_eq = part(940, [CT, CT])
        earlier = part(1565, [CT, CT])
        base_tab = part(2190, [NB + 2, NB])
        table = part(2865, [KEYS])
        found = xs3[0][0:B, :, :, :].rearrange("p a b d -> p (a b d)").bitcast(F32)[:, 0:CT * KEYS].rearrange("p (j b) -> p j b", b=KEYS)
        r_t = part(2940, [8, CT])
        nov = sb("nov", [128, 4])
        nov_i = sb("nov_i", [1, 1], I32)
        fb = sb("fb", [128, 6, 30])
        kb = sb("kb", [B, B])
        kcol = sb("kcol", [B, 4])
        v3 = sb("v3", [B, 3])
        s3 = sb("s3", [B, 3])
        same = sb("same", [B, B])
        same_tri = sb("same_tri", [B, B])
        rank1 = sb("rank1", [B, 1])
        idx = sb("idx", [B, 1], I32)
        ohoff = sb("ohoff", [B, B], BF16)
        ohdb = sb("ohdb", [B, NB])
        frow = sb("frow", [B, F])
        rhs12 = sb("rhs12", [B, NB, F], BF16)
        counts = sb("counts", [B, NB, FN])
        countsT = sb("countsT", [FN, N])
        halfdeg = sb("halfdeg", [B, NB])
        r0 = sb("r0", [FN, D])
        r1 = sb("r1", [FN, D])
        r3 = sb("r3", [FN, D])
        mem_c = sb("mem_c", [D, 1])
        wih0_s = sb("wih0_s", [D, 3 * D])
        b0 = sb("b0", [D, 2, 3])
        gru = sb("gru", [D, 10])
        wtb_s = sb("wtb_s", [D, D])
        nwT = sb("nwT", [D, D])
        w1 = sb("w1", [D, 3, D])
        wmsg_s = sb("wmsg_s", [D, D])
        wih_s = sb("wih_s", [D, 3 * D])
        whh_s = sb("whh_s", [D, 3 * D])
        b3 = sb("b3", [D, 2, 3])
        b3s = sb("b3s", [D, 3])
        agg = part(0, [GW], lanes=D)
        hT = part(GW, [GW], lanes=D)
        mT = cT[:, 4 * GW:5 * GW]
        gr = cT[:, 0:4 * GW].rearrange("p (n w) -> p n w", w=GW)
        y, yc, sq = (part(2 * GW + n * GB * D, [GB, D]) for n in range(3))
        st = sb("st", [B, 4, GB])
        epsc = sb("epsc", [128, 1])
        mark = sb("mark", [1, 1])
        mark2 = sb("mark2", [1, 1])

        row_c = ring[:, 0, 0:GB * GW].bitcast(BF16).rearrange("p (r m n) -> p r m n", r=GB, m=2)
        row_s = ring[:, 1, 0:GB * GW].rearrange("p (r n) -> p r n", r=GB)
        back = ring[:, 2:4, :].rearrange("p a n -> p (a n)")
        bk = back[:, 0:KC * SLOTS * 2].rearrange("p (k s e) -> p k s e", k=KC, e=2)
        ohs = back[:, 5504:5504 + OHR * 64].bitcast(BF16).rearrange("p (o n) -> p o n", o=OHR)
        ohd = back[:, 3904:3904 + 1600].bitcast(BF16)[:, 0:OHR * 5 * B].rearrange("p (o m n) -> p o m n", o=OHR, m=5)
        featc = back.bitcast(BF16)[:, 0:SLOTS * F].rearrange("p (s f) -> p s f", f=F)
        fields = xs3[1][:, :, :, :].rearrange("p a b d -> p (a b d)").bitcast(F32)
        fld = fields[:, 0:6 * SLOTS].rearrange("p (n s) -> p n s", s=SLOTS)
        zero = fields[:, 0:2 * SLOTS]

        bank_sets = [ctx.enter_context(nc.psum_tensor(f"banks{i}", [128, 3, 512], F32)) for i in range(2)]
        acc = [bank_sets[0][:, 0, :], bank_sets[0][:, 1, :]]
        dn = [bank_sets[0][:, 2, :], bank_sets[1][:, 0, :]]
        tp = [bank_sets[1][:, 1, :], bank_sets[1][:, 2, :]]
        cnt = pb("cnt")
        gx = pb("gx")
        sets = [[acc[0], acc[1], dn[0]], [dn[1], tp[0], tp[1]]]

        names = """ld_edges ld_x ld_w ld_q zeroed iota_done consts prod_done square_done sums_done norm_in norm_out
            attr_in0 attr_in1 oh_ready table_ps0 table_ps1 ps_free slots_ready prefilled bucket_in
            nov_in nov_ps nov_ready fields_ready row_init oh_full oh_used group_ps evac rows_ready built
            tile_ready keyrow same_ready tile_sums idx_ready tile_done over_zero over_zero_b over_in over_used fbv
            cnt_init counts_psum counts_sb countsT_ps countsT_sb q_ssq q_norm q_ready
            gi gru_ready0 gru_rz gru_t gru_n u_ready wt_in0 wt_in1 wt_used nw_ready w_small
            acc_free h_ready lin_ready lin_free xc_ready sq_ready sd_in sd_ready x_ready split_ready
            t_ready t_free tr_ready tr_free msg_ready m_ready gates_ready rz_ready n_in n_ready
            yT_ready yt_ready y_ready out_done piece_used dve agg_used x2_ready""".split()
        S = {n: sem(n) for n in names}
        piece_in = [sem(f"piece_in{k}") for k in range(RING)]
        scat = [sem(f"scat{k}") for k in range(KC)]
        oscat = [sem(f"oscat{k}") for k in range(3)]
        row_out = [sem(f"row_out{r}") for r in range(GB)]

        attr_v = attr.rearrange("(c p j) d -> c p j d", p=B, j=CT)
        attr_buf = [ring[0:B, i, :].rearrange("p (t d) -> p t d", d=D) for i in range(2)]
        prod = ring[0:B, 2, :].rearrange("p (t d) -> p t d", d=D)
        squa = ring[0:B, 3, :].rearrange("p (t d) -> p t d", d=D)
        L0, L1A, L1B, L2A, L2B, L3 = range(6)
        PASSES = [(COUNT, xs3[0]), (COUNT, xs3[1]), (CTRL, xs3[1]), (SIM, xc), (SIM, xa), (COUNT, xs3[0])]

        CPASS = {L0: 0, L1A: 1, L1B: 2, L3: 3}

        block = ctx.enter_context(nc.Block())

        def piece_loop(eng, body):
            with eng.Fori(0, G - 1) as a:
                body(6 * a, True, 155 * a)
                with eng.Fori(0, G) as b:
                    body(6 * a + b + 1, False, 155 * a + 25 * b + 30)
            body(24, True, 620)

        def tiles_of(r, diagonal):
            return [[5 * r + c] + ([25 + r] if diagonal and c == r else []) for c in range(GB)]

        def row_order(r, diagonal):
            n, at = sum(len(t) for q in range(r) for t in tiles_of(q, diagonal)), []
            for c, t in enumerate(tiles_of(r, diagonal)):
                at.append([(n + i, col) for i, col in enumerate(t)])
                n += len(t)
            return at

        @block.sync
        def _(sp):
            for n, a in enumerate((dst, src, ty2, ty9)):
                sp.dma_start(ei[:, n, :].rearrange("p (c j) -> p c j", j=CT), a.rearrange("(c p j) -> p c j", p=B, j=CT))\
                    .then_inc(S["ld_edges"], 16)
            sp.dma_start(q_bc[:, :], quest.partition_broadcast(B).rearrange("p a d -> p (a d)")).then_inc(S["ld_q"], 16)
            sp.wait_ge(S["zeroed"], 1)
            for k in range(KC):
                sp.dma_start(buckets[k].rearrange("(p s) e -> p (s e)", p=LANES), zero).then_inc(S["prefilled"], 16)
            for c in range(NCH):
                if c >= 2:
                    sp.wait_ge(S["prod_done"], c - 1)
                    sp.wait_ge(S["square_done"], c - 1)
                for lo, hi in ((0, 112), (112, B)):
                    sp.dma_start(attr_buf[c % 2][lo:hi], attr_v[c, lo:hi]).then_inc(S[f"attr_in{c % 2}"], 16)
                if c == 1:
                    sp.dma_start(xa[0:B, :, :], x.rearrange("(b p) d -> p b d", p=B)).then_inc(S["ld_x"], 16)
            sp.wait_ge(S["sums_done"], NCH)
            for k in range(KC):
                sp.wait_ge(scat[k], 16 * len(range(k, T, KC)))
                sp.dma_start(bk[:, k, :, :], buckets[k].rearrange("(p s) e -> p s e", p=LANES)).then_inc(S["bucket_in"], 16)

            def rows(piece, diagonal, _):
                for r in range(GB):
                    sp.wait_ge(S["rows_ready"], 4 * (GB * piece + r + 1) + 4)
                    for m in range(2):
                        sp.dma_start(dense_v[m][bass.ds(piece, 1), :, r * GW:(r + 1) * GW].rearrange("a p n -> (a p) n"),
                                     row_c[:, r, m, :]).then_inc(row_out[r], 16)
                    sp.dma_start(dense_v[SIM][bass.ds(piece, 1), :, r * GW:(r + 1) * GW].rearrange("a p n -> (a p) n"),
                                 row_s[:, r, :]).then_inc(row_out[r], 16)

            piece_loop(sp, rows)
            for r in range(GB):
                sp.wait_ge(row_out[r], 48 * (NPIECE + 1))
            sp.sem_inc(S["built"], 1)
            sp.wait_ge(S["nov_ready"], 1)
            over_n = sp.value_load(nov_i[0:1, 0:1], min_val=0, max_val=E)
            with sp.If(over_n > 0):
                sp.wait_ge(S["over_zero"], 1)
                for m in range(2):
                    for q in range(NPIECE):
                        for r in range(GB):
                            sp.dma_start(over_v[m][q][:, r * GW:(r + 1) * GW], obuf[:, :]).then_inc(S["over_zero_b"], 16)
                for m in range(3):
                    sp.wait_ge(oscat[m], 16 * T)
            for n, (m, _) in enumerate(PASSES):
                for g in range(G):
                    if m != SIM:
                        with sp.If(over_n > 0):
                            for s in range(NB):
                                at = (CPASS[n] * G + g) * NB + s
                                if at:
                                    sp.wait_ge(S["over_used"], at)
                                k, r = divmod(s, GB)
                                sp.dma_start(obuf[:, :], over_v[m][g * G + k][:, r * GW:(r + 1) * GW]).then_inc(S["over_in"], 16)
                    for k in range(G):
                        at = (n * G + g) * G + k
                        if at >= RING:
                            sp.wait_ge(S["piece_used"], at - RING + 1)
                        elif at == 2:
                            sp.wait_ge(S["counts_psum"], 1)
                        to = ring[:, at % RING, 0:PIECE] if m == SIM else ring[:, at % RING, 0:ROW // 2].bitcast(BF16)[:, 0:PIECE]
                        sp.dma_start(to, dense_v[m][g * G + k][:, 0:PIECE]).then_inc(piece_in[at % RING], 16)
            out_v = out.rearrange("(b p) d -> p b d", p=B)
            for g in range(G):
                sp.wait_ge(S["x_ready"], 3 * G + g + 1)
                sp.dma_start(out_v[:, g * GB:(g + 1) * GB, :], xa[0:B, g * GB:(g + 1) * GB, :]).then_inc(S["out_done"], 16)
            sp.wait_ge(S["out_done"], 16 * G)

        @block.gpsimd
        def _(pool):
            nc.gpsimd.iota(iot_i[:, 0:128], pattern=[[1, 128]], base=0, channel_multiplier=0).then_inc(S["iota_done"], 1)
            nc.gpsimd.iota(iot_i[:, 128:129], pattern=[[1, 1]], base=0, channel_multiplier=1).then_inc(S["iota_done"], 1)
            nc.gpsimd.memset(zero, 0.0).then_inc(S["zeroed"], 1)
            pool.wait_ge(S["prefilled"], 16 * KC)
            for t in range(T):
                if t % CT == 0:
                    pool.wait_ge(S["slots_ready"], t // CT + 1)
                if t >= KC:
                    pool.wait_ge(scat[t % KC], 16 * (t // KC))
                nc.gpsimd.indirect_dma_start(
                    buckets[t % KC], bass.IndirectOffsetOnAxis(ap=slot[:, t:t + 1], axis=0), rec[:, t, :], None,
                    bounds_check=LANES * SLOTS - 1, oob_is_err=False).then_inc(scat[t % KC], 16)
            pool.wait_ge(S["nov_ready"], 1)
            over_n = pool.value_load(nov_i[0:1, 0:1], min_val=0, max_val=E)
            with pool.If(over_n > 0):
                pool.wait_ge(S["built"], 1)
                nc.gpsimd.memset(obuf[:, :], 0.0).then_inc(S["over_zero"], 1)
                pool.wait_ge(S["over_zero_b"], 16 * 2 * NPIECE * GB)
                nc.gpsimd.memset(mark[:, :], 0.0).then_inc(S["tile_done"], 1)
                last_elem = pool.to_reg(ELEMS + 127)
                with pool.Fori(0, T) as t:
                    pool.wait_ge(S["idx_ready"], t + 1)
                    nc.gpsimd.tensor_tensor(mark[:, :], kcol[0:1, 0:1], kcol[0:1, 0:1], ALU.add)\
                        .then_inc(S["tile_done"], 1)
                    for m in range(3):
                        nc.gpsimd.indirect_dma_start(
                            over_dst[m], bass.IndirectOffsetOnAxis(ap=idx[:, 0:1], axis=0), s3[:, m:m + 1], None,
                            bounds_check=last_elem, oob_is_err=True, compute_op=ALU.add).then_inc(oscat[m], 16)

        @block.scalar
        def _(act):
            small = [(mem_c[:, :], mem), (wih0_s[:, :], wih0), (b0[:, 0, :], bih0), (b0[:, 1, :], bhh0), (wtb_s[:, :], wtb),
                     (w1[:, 0, :], wd), (w1[:, 1, :], wc), (w1[:, 2, :], ws), (wmsg_s[:, :], wmsg), (wih_s[:, :], wih),
                     (whh_s[:, :], whh), (b3[:, 0, :], bih), (b3[:, 1, :], bhh)]
            for o, i in small:
                act.dma_start(o, i).then_inc(S["ld_w"], 16)
            act.wait_ge(S["w_small"], 1)
            for o, i in ((r0[12:13, :], linb), (r1[0:1, :], bd), (r1[1:2, :], bc), (r1[12:13, :], bs), (r3[2:3, :], bmsg)):
                act.dma_start(o, i.rearrange("(a d) -> a d", a=1)).then_inc(S["ld_w"], 16)
            act.dma_start(r3[3:12, :], embed).then_inc(S["ld_w"], 16)
            act.wait_ge(S["q_ssq"], 1)
            nc.scalar.activation(q_s[:, 1:2], q_s[:, 0:1], ACT.Sqrt).then_inc(S["q_norm"], 1)
            act.wait_ge(S["gi"], 1)
            act.wait_ge(S["gru_ready0"], 1)
            for k in range(2):
                nc.scalar.activation(gru[:, k:k + 1], gx[:, k:k + 1], ACT.Sigmoid, bias=gru[:, 6 + k:7 + k]).then_inc(S["gru_rz"], 1)
            act.wait_ge(S["gru_t"], 1)
            nc.scalar.activation(gru[:, 4:5], gru[:, 3:4], ACT.Tanh).then_inc(S["gru_n"], 1)
            for c in range(NCH + 1):
                if c < NCH:
                    act.wait_ge(S[f"attr_in{c % 2}"], 32 * (c // 2 + 1))
                    if c >= 1:
                        act.wait_ge(S["sums_done"], c)
                    nc.scalar.activation(squa, attr_buf[c % 2], ACT.Square).then_inc(S["square_done"], 1)
                    if c < 16:
                        if c >= 2:
                            act.wait_ge(S["wt_used"], c - 1)
                        act.dma_start(wtr[:, c % 2, :], wt[:, c * 1024:(c + 1) * 1024]).then_inc(S[f"wt_in{c % 2}"], 16)
                if c >= 1:
                    act.wait_ge(S["norm_in"], c)
                    nc.scalar.activation(normr[:, (c - 1) % 2, :], norm2[:, (c - 1) % 2, :], ACT.Sqrt).then_inc(S["norm_out"], 1)

            act.wait_ge(S["row_init"], 2)
            for r in range(GB):
                act.sem_inc(row_out[r], 48)
            act.sem_inc(S["rows_ready"], 4)

            def evacuate(piece, diagonal, _):
                for r in range(GB):
                    act.wait_ge(row_out[r], 48 * (piece + 1))
                    for h, (lo, hi) in enumerate(((0, 3), (3, 5))):
                        act.wait_ge(S["group_ps"], 10 * piece + 2 * r + h + 1)
                        ps = bank_sets[h][0:B, 0:hi - lo, :]
                        nc.scalar.copy(row_c[0:B, r, :, lo * B:hi * B].rearrange("p m (c n) -> p c m n", n=B),
                                       ps[:, :, 0:2 * B].rearrange("p c (m n) -> p c m n", m=2)).then_inc(S["rows_ready"], 1)
                        nc.scalar.copy(row_s[0:B, r, lo * B:hi * B].rearrange("p (c n) -> p c n", n=B),
                                       ps[:, :, 2 * B:3 * B]).then_inc(S["rows_ready"], 1)

            piece_loop(act, evacuate)
            for b in range(NB):
                act.wait_ge(S["countsT_ps"], b + 1)
                nc.scalar.copy(countsT[:, b * B:(b + 1) * B], tp[b % 2][0:FN, 0:B]).then_inc(S["countsT_sb"], 1)

            def transposed(turn):
                for c in range(7):
                    act.wait_ge(S["t_ready"], turn * 7 + c + 1)
                    lo, hi = c * 4, min(NB, c * 4 + 4)
                    nc.scalar.copy(xT[:, lo * B:hi * B], tp[c % 2][:, 0:(hi - lo) * B]).then_inc(S["t_free"], 1)

            USED = {L0: 0, L1B: G, L2A: 2 * G, L2B: 3 * G, L3: 4 * G}

            def group_out(n, g, to):
                act.wait_ge(S["piece_used"], G * (n * G + g + 1))
                if n != L1A and USED[n] + g > 0:
                    act.wait_ge(S["agg_used"], USED[n] + g)
                for h in range(2):
                    nc.scalar.copy(to[:, h * HALF[0]:h * HALF[0] + HALF[h]], acc[h][:, 0:HALF[h]]).then_inc(S["acc_free"], 1)

            def norm_part(k):
                act.wait_ge(S["xc_ready"], k + 1)
                nc.scalar.activation(sq[:, :, :], yc[:, :, :], ACT.Square).then_inc(S["sq_ready"], 1)
                act.wait_ge(S["sd_in"], k + 1)
                nc.scalar.activation(st[:, 2, :], st[:, 1, :], ACT.Sqrt, bias=epsc[0:B, 0:1], scale=1.0 / D).then_inc(S["sd_ready"], 1)

            transposed(0)
            for g in range(G):
                group_out(L0, g, agg)
                norm_part(g)
            transposed(1)
            for g in range(G):
                group_out(L1A, g, cT[:, g * GW:(g + 1) * GW])
            for g in range(G):
                group_out(L1B, g, agg)
                norm_part(G + g)
            for g in range(G):
                group_out(L2A, g, agg)
            for g in range(G):
                group_out(L2B, g, agg)
                norm_part(2 * G + g)
            transposed(2)
            for g in range(G):
                group_out(L3, g, agg)
                for h in range(2):
                    w, lo = HALF[h], h * HALF[0]
                    act.wait_ge(S["msg_ready"], 2 * g + h + 1)
                    nc.scalar.copy(mT[:, lo:lo + w], dn[h][:, 0:w]).then_inc(S["m_ready"], 1)
                    act.wait_ge(S["gates_ready"], 2 * g + h + 1)
                    for k in range(2):
                        nc.scalar.activation(gr[:, k, lo:lo + w], tp[k][:, 0:w], ACT.Sigmoid, bias=b3s[:, k:k + 1]).then_inc(S["rz_ready"], 1)
                    act.wait_ge(S["n_in"], 2 * g + h + 1)
                    nc.scalar.activation(gr[:, 2, lo:lo + w], gr[:, 3, lo:lo + w], ACT.Tanh, bias=b3[:, 0, 2:3]).then_inc(S["n_ready"], 1)
                act.wait_ge(S["yt_ready"], g + 1)
                nc.scalar.copy(y[:, 0:4, :], dn[0][0:B, :].rearrange("p (b d) -> p b d", d=D)).then_inc(S["y_ready"], 1)
                nc.scalar.copy(y[:, 4, :], dn[1][0:B, 0:D]).then_inc(S["y_ready"], 1)
                norm_part(3 * G + g)

        @block.tensor
        def _(pe):
            pe.sem_inc(S["oh_used"], OHR)
            pe.wait_ge(S["ld_w"], 16 * 19)
            for k in range(3):
                last = nc.tensor.matmul(gx[:, k:k + 1], wih0_s[:, k * D:(k + 1) * D], mem_c[:, :], start=True, stop=True)
            last.then_inc(S["gi"], 1)
            pe.wait_ge(S["consts"], 1)
            for c in range(NCH):
                pe.wait_ge(S["oh_ready"], c + 1)
                for m, w in ((0, before[:, :]), (1, ones_bf[0:B, 0:B])):
                    for j in range(CT):
                        last = nc.tensor.matmul(acc[m][0:B, 0:KEYS], w, oh[:, j, :], start=(j == 0), stop=(j == CT - 1))
                    last.then_inc(S["table_ps0"], 1)
                if c == 0:
                    pe.wait_ge(S["u_ready"], 1)
                if c < 16:
                    pe.wait_ge(S[f"wt_in{c % 2}"], 16 * (c // 2 + 1))
                    for o in range(8):
                        last = nc.tensor.matmul(dn[1][:, c * 8 + o:c * 8 + o + 1], wtr[:, c % 2, o * D:(o + 1) * D], gru[:, 5:6],
                                                start=True, stop=True)
                    last.then_inc(S["wt_used"], 1)
            pe.wait_ge(S["nov_in"], 1)
            nc.tensor.matmul(gx[0:1, 8:9], nov[0:B, 0:1], nov[0:B, 1:2], start=True, stop=True).then_inc(S["nov_ps"], 1)
            nc.tensor.matmul(cnt[0:B, 0:NB * F], zrow[0:B, 0:B], zrow[0:B, 0:NB * F], start=True, stop=False,
                             skip_group_check=True).then_inc(S["cnt_init"], 1)
            pe.wait_ge(S["cnt_init"], 1)
            pe.wait_ge(S["nw_ready"], 1)

            def blocks(piece, diagonal, before_n):
                db0 = (piece * 13) // 64 * GB if isinstance(piece, int) else ((piece * 13) >> 6) * GB
                for r in range(GB):
                    for c, tiles in enumerate(row_order(r, diagonal)):
                        h = c // 3
                        ps = sets[h][c - 3 * h]
                        if c % 3 == 0:
                            pe.wait_ge(S["rows_ready"], 20 * piece + 4 * r + 2 * h + 2)
                        for i, (n, col) in enumerate(tiles):
                            o = n % OHR
                            pe.wait_ge(S["oh_full"], before_n + n + 1)
                            end = i == len(tiles) - 1
                            nc.tensor.matmul(ps[0:B, 0:3 * B], ohs[:, o, 0:B], ohd[:, o, 0:3, :].rearrange("p m n -> p (m n)"),
                                             start=(i == 0), stop=False, skip_group_check=True)
                            nc.tensor.matmul(ps[0:B, 2 * B:3 * B], ohs[:, o, 0:B], ohd[:, o, 3, :], start=False, stop=False,
                                             skip_group_check=True)
                            last = nc.tensor.matmul(ps[0:B, 2 * B:3 * B], ohs[:, o, 0:B], ohd[:, o, 4, :], start=False, stop=end,
                                                    skip_group_check=True)
                            if end and c in (2, 4):
                                last.then_inc(S["group_ps"], 1)
                            src_col = 25 * piece + col if col < 25 else 625 + db0 + (col - 25)
                            last = nc.tensor.matmul(cnt[0:B, bass.ds((db0 + c) * F, F)], ohd[:, o, 0, :],
                                                    featc[:, bass.ds(src_col, 1), :].rearrange("p a f -> p (a f)"),
                                                    start=False, stop=False, skip_group_check=True)
                            last.then_inc(S["oh_used"], 1)

            piece_loop(pe, blocks)
            pe.wait_ge(S["nov_ready"], 1)
            over_n = pe.value_load(nov_i[0:1, 0:1], min_val=0, max_val=E)
            with pe.If(over_n > 0):
                with pe.Fori(0, T) as t:
                    pe.wait_ge(S["tile_ready"], t + 1)
                    nc.tensor.transpose(tp[0][0:B, 0:B], kb[:, :], ident[0:B, 0:B]).then_inc(S["keyrow"], 1)
                    nc.tensor.matmul(cnt[0:B, 0:NB * F], ohoff[:, :], rhs12[:, :, :].rearrange("p b f -> p (b f)"),
                                     start=False, stop=False, skip_group_check=True)
                    pe.wait_ge(S["same_ready"], t + 1)
                    nc.tensor.matmul(tp[1][0:B, 0:3], same[:, :], v3[:, :], start=True, stop=True).then_inc(S["tile_sums"], 1)
            nc.tensor.matmul(cnt[0:B, 0:NB * F], zrow[0:B, 0:B], zrow[0:B, 0:NB * F], start=False, stop=True,
                             skip_group_check=True).then_inc(S["counts_psum"], 1)
            pe.wait_ge(S["rows_ready"], 20 * NPIECE + 4)
            pe.wait_ge(S["counts_sb"], 1)
            for b in range(NB):
                if b >= 2:
                    pe.wait_ge(S["countsT_sb"], b - 1)
                nc.tensor.transpose(tp[b % 2][0:FN, 0:B], counts[:, b, :], ident[0:B, 0:B]).then_inc(S["countsT_ps"], 1)
            pe.wait_ge(S["countsT_sb"], NB)

            def transposes(turn, xs):
                for c in range(7):
                    if turn * 7 + c >= 2:
                        pe.wait_ge(S["t_free"], turn * 7 + c - 1)
                    for b in range(c * 4, min(NB, c * 4 + 4)):
                        last = nc.tensor.transpose(tp[c % 2][:, (b % 4) * B:(b % 4 + 1) * B], xs[0:B, b, :], ident[0:B, 0:B])
                    last.then_inc(S["t_ready"], 1)

            def aggregate(n, g):
                m, xs = PASSES[n]
                if n * G + g >= 1:
                    pe.wait_ge(S["acc_free"], 2 * (n * G + g))
                if m != SIM:
                    for h in range(2):
                        nc.tensor.matmul(acc[h][:, 0:HALF[h]], zrow[0:B, 0:128], zrow[0:B, 0:HALF[h]], start=True, stop=False,
                                         skip_group_check=True)
                    xf = {L0: xa, L1A: xb, L1B: xb, L3: xb}[n]
                    with pe.If(over_n > 0):
                        for s in range(NB):
                            pe.wait_ge(S["over_in"], 16 * ((CPASS[n] * G + g) * NB + s + 1))
                            for h in range(2):
                                lo = h * HALF[0]
                                last = nc.tensor.matmul(acc[h][:, 0:HALF[h]], xf[0:B, s, :], obuf[0:B, lo:lo + HALF[h]],
                                                        start=False, stop=False, skip_group_check=True)
                            last.then_inc(S["over_used"], 1)
                for k in range(G):
                    at = (n * G + g) * G + k
                    pe.wait_ge(piece_in[at % RING], 16 * (at // RING + 1))
                    for r in range(GB):
                        s = k * GB + r
                        for p3 in range(1 if m == SIM else 3):
                            for h in range(2):
                                lo = r * GW + h * HALF[0]
                                if m == SIM:
                                    last = nc.tensor.matmul(acc[h][:, 0:HALF[h]], xs[0:B, s, :], ring[0:B, at % RING, lo:lo + HALF[h]],
                                                            start=(s == 0), stop=(s == NB - 1))
                                else:
                                    rhs = ring[0:B, at % RING, 0:ROW // 2].bitcast(BF16)[:, lo:lo + HALF[h]]
                                    last = nc.tensor.matmul(acc[h][:, 0:HALF[h]], xs[0:B, p3, s, :], rhs, start=False,
                                                            stop=(s == NB - 1 and p3 == 2), skip_group_check=True)
                    last.then_inc(S["piece_used"], 1)

            def linear(k, g, terms, bias):
                pe.wait_ge(S["h_ready"], k * G + g + 1)
                if k * G + g >= 1:
                    pe.wait_ge(S["lin_free"], k * G + g)
                for b in range(GB):
                    o = dn[b // 4][0:B, (b % 4) * D:(b % 4 + 1) * D]
                    for i, (lhs, base, w) in enumerate(terms):
                        nc.tensor.matmul(o, lhs[:, (base + b) * B:(base + b + 1) * B], w, start=(i == 0), stop=False)
                    last = nc.tensor.matmul(o, countsT[:, (g * GB + b) * B:(g * GB + b + 1) * B], bias, start=False, stop=True)
                last.then_inc(S["lin_ready"], 1)

            pe.wait_ge(S["ld_x"], 16)
            transposes(0, xa)
            pe.wait_ge(S["split_ready"], G)
            for g in range(G):
                aggregate(L0, g)
                linear(0, g, [(hT, 0, nwT[:, :])], r0[:, :])
            pe.wait_ge(S["split_ready"], 2 * G)
            transposes(1, xb)
            for g in range(G):
                aggregate(L1A, g)
            for g in range(G):
                aggregate(L1B, g)
                linear(1, g, [(hT, 0, w1[:, 0, :]), (agg, 0, w1[:, 1, :]), (xT, g * GB, w1[:, 2, :])], r1[:, :])
            pe.wait_ge(S["x_ready"], 2 * G)
            for n in (L2A, L2B):
                if n == L2B:
                    pe.wait_ge(S["x2_ready"], G)
                for g in range(G):
                    aggregate(n, g)
                    pe.wait_ge(S["acc_free"], 2 * (n * G + g + 1))
                    if g or n == L2B:
                        pe.wait_ge(S["tr_free"], (n - L2A) * G + g)
                    for b in range(GB):
                        last = nc.tensor.transpose(dn[b // 4][0:B, (b % 4) * D:(b % 4 + 1) * D], agg[:, b * B:(b + 1) * B], ident[:, :])
                    last.then_inc(S["tr_ready"], 1)
            pe.wait_ge(S["split_ready"], 3 * G)
            transposes(2, xb)
            for g in range(G):
                aggregate(L3, g)
                pe.wait_ge(S["acc_free"], 2 * (L3 * G + g + 1))
                if g:
                    pe.wait_ge(S["y_ready"], 2 * g)
                for h in range(2):
                    w, lo = HALF[h], h * HALF[0]
                    nc.tensor.matmul(dn[h][:, 0:w], wmsg_s[:, :], agg[:, lo:lo + w], start=True, stop=False)
                    nc.tensor.matmul(dn[h][:, 0:w], r3[:, :], countsT[:, g * GW + lo:g * GW + lo + w],
                                     start=False, stop=True).then_inc(S["msg_ready"], 1)
                for h in range(2):
                    w, lo = HALF[h], h * HALF[0]
                    m, hh = mT[:, lo:lo + w], xT[:, g * GW + lo:g * GW + lo + w]
                    pe.wait_ge(S["m_ready"], 2 * g + h + 1)
                    if g or h:
                        pe.wait_ge(S["rz_ready"], 2 * (2 * g + h))
                        pe.wait_ge(S["n_in"], 2 * g + h)
                    else:
                        pe.wait_ge(S["t_free"], 21)
                    for k in range(2):
                        nc.tensor.matmul(tp[k][:, 0:w], wih_s[:, k * D:(k + 1) * D], m, start=True, stop=False)
                        nc.tensor.matmul(tp[k][:, 0:w], whh_s[:, k * D:(k + 1) * D], hh, start=False, stop=True)
                    nc.tensor.matmul(gx[:, 0:w], wih_s[:, 2 * D:3 * D], m, start=True, stop=True)
                    nc.tensor.matmul(cnt[:, 0:w], whh_s[:, 2 * D:3 * D], hh, start=True, stop=True).then_inc(S["gates_ready"], 1)
                pe.wait_ge(S["yT_ready"], 2 * (g + 1))
                for b in range(GB):
                    last = nc.tensor.transpose(dn[b // 4][0:B, (b % 4) * D:(b % 4 + 1) * D], hT[:, b * B:(b + 1) * B], ident[:, :])
                last.then_inc(S["yt_ready"], 1)

        @block.vector
        def _(dve):
            v = nc.vector
            step = Steps(dve, S["dve"])
            step(v.memset(r0[:, :], 0.0))
            step(v.memset(r1[:, :], 0.0))
            step(v.memset(epsc[:, :], EPS))
            v.memset(r3[:, :], 0.0).then_inc(S["w_small"], 1)
            step(v.memset(zrow[:, :], 0.0))
            step(v.memset(ones_bf[:, :], 1.0))
            step(v.memset(base_tab[:, :, :], 0.0))
            step(v.memset(counts[:, :, :], 1.0))
            step(v.memset(nov[:, :], 1.0))
            dve.wait_ge(S["iota_done"], 2)
            step(v.tensor_copy(iot[:, :], iot_i[:, :]))
            step(v.tensor_copy(iota_bf[:, :], iot_i[:, 0:128]))
            lane = iot[:, 128:129]
            step(v.tensor_scalar(ident[:, :], iot[:, 0:128], lane, None, ALU.is_equal))
            step(v.tensor_scalar(before[:, :], iot[0:B, 0:B], lane[0:B], None, ALU.is_gt))
            step(v.tensor_tensor(earlier[:, :, :], iot[0:B, 0:CT].unsqueeze(1).to_broadcast([B, CT, CT]),
                                 iot[0:B, 0:CT].unsqueeze(2).to_broadcast([B, CT, CT]), ALU.is_lt))
            v.tensor_scalar(tri[:, :], iot[:, 0:128], lane, None, ALU.is_lt).then_inc(S["consts"], 1)
            dve.wait_ge(S["ld_q"], 16)
            step(v.tensor_tensor(q_n[:, :], q_bc[:, :], q_bc[:, :], ALU.mult))
            step(v.tensor_reduce(q_s[:, 2:3], q_n[:, :], AXX, ALU.add))
            v.tensor_scalar(q_s[:, 0:1], q_s[:, 2:3], 1e-24, None, ALU.max).then_inc(S["q_ssq"], 1)
            dve.wait_ge(S["q_norm"], 1)
            step(v.reciprocal(q_s[:, 3:4], q_s[:, 1:2]))
            v.tensor_scalar(q_n[:, :], q_bc[:, :], q_s[:, 3:4], None, ALU.mult).then_inc(S["q_ready"], 1)
            dve.wait_ge(S["q_ready"], 1)
            dve.wait_ge(S["ld_w"], 16 * 19)
            step(v.tensor_tensor(b3s[:, :], b3[:, 0, :], b3[:, 1, :], ALU.add))
            v.tensor_tensor(gru[:, 6:8], b0[:, 0, 0:2], b0[:, 1, 0:2], ALU.add).then_inc(S["gru_ready0"], 1)
            dve.wait_ge(S["gru_rz"], 2)
            step(v.tensor_tensor(gru[:, 2:3], gru[:, 0:1], b0[:, 1, 2:3], ALU.mult))
            step(v.tensor_tensor(gru[:, 2:3], gru[:, 2:3], b0[:, 0, 2:3], ALU.add))
            v.tensor_tensor(gru[:, 3:4], gru[:, 2:3], gx[:, 2:3], ALU.add).then_inc(S["gru_t"], 1)
            step(v.tensor_scalar(gru[:, 8:9], gru[:, 1:2], -1.0, 1.0, ALU.mult, ALU.add))
            dve.wait_ge(S["gru_n"], 1)
            v.tensor_tensor(gru[:, 5:6], gru[:, 8:9], gru[:, 4:5], ALU.mult).then_inc(S["u_ready"], 1)

            dve.wait_ge(S["ld_edges"], 64)
            dstf, srcf, t2, t9, db, sbl, dg, sk, do, so, key, tmp, key3, caps = ef
            bid, place, more = efx
            for n in range(4):
                step(v.tensor_copy(ef[n], ei[:, n, :]))

            def floor_div(o, i, by, t, mul=1.0, plus=0.0):
                step(v.tensor_scalar(t, i, mul / by, (plus + 0.5) / by - 0.5, ALU.mult, ALU.add))
                step(v.tensor_scalar(o, t, MAGIC, -MAGIC, ALU.add, ALU.add))

            floor_div(db, dstf, B, tmp)
            floor_div(sbl, srcf, B, tmp)
            floor_div(dg, dstf, GW, tmp)
            floor_div(sk, sbl, GB, tmp)
            step(v.scalar_tensor_tensor(do, db, -float(B), dstf, ALU.mult, ALU.add))
            step(v.scalar_tensor_tensor(so, sbl, -float(B), srcf, ALU.mult, ALU.add))
            step(v.scalar_tensor_tensor(key, dg, float(G), sk, ALU.mult, ALU.add))
            step(v.scalar_tensor_tensor(key, key, 128.0, so, ALU.mult, ALU.add))
            step(v.scalar_tensor_tensor(key, key, float(ROW), dstf, ALU.mult, ALU.add))
            step(v.scalar_tensor_tensor(key, dg, -float(GW), key, ALU.mult, ALU.add))
            step(v.scalar_tensor_tensor(tmp, sk, -float(GB), sbl, ALU.mult, ALU.add))
            step(v.scalar_tensor_tensor(key, tmp, float(GW), key, ALU.mult, ALU.add))
            step(v.tensor_scalar(t9, t9, 0.0, 8.0, ALU.max, ALU.min))
            step(v.tensor_scalar(t2, t2, 0.0, None, ALU.not_equal))
            step(v.scalar_tensor_tensor(bid, db, float(NB), sbl, ALU.mult, ALU.add))
            step(v.scalar_tensor_tensor(place, sbl, float(GB), db, ALU.mult, ALU.add))
            step(v.scalar_tensor_tensor(place, dg, float(NB * GB - GB), place, ALU.mult, ALU.add))
            step(v.tensor_scalar(more, sbl, float(NB * NB - LANES * SLOTS), None, ALU.add))
            step(v.tensor_tensor(more, more, place, ALU.subtract))
            floor_div(winoff[:, 1, :], iot[0:B, 0:NCH], float(NCH), winoff[:, 0, :], float(NB), 13.0)
            d3, k3, c3, s3b, p3b = (a.rearrange("p (c j) -> p c j", j=CT) for a in (db, key3, caps, sbl, tmp))
            w3 = winoff[:, 1, :].unsqueeze(2).to_broadcast([B, NCH, CT])
            step(v.tensor_tensor(p3b, d3, w3, ALU.subtract))
            step(v.tensor_scalar(tmp, tmp, 1.0, None, ALU.add))
            step(v.scalar_tensor_tensor(key3, tmp, float(NB), sbl, ALU.mult, ALU.add))
            step(v.tensor_tensor(caps, db, sbl, ALU.is_equal))
            step(v.tensor_scalar(caps, caps, 128.0, 128.0, ALU.mult, ALU.add))
            step(v.tensor_scalar(tmp, tmp, 1.0, None, ALU.subtract))
            step(v.tensor_tensor(tmp, tmp, tmp, ALU.mult))
            step(v.tensor_scalar(tmp, tmp, 1.5, -1000.0, ALU.is_gt, ALU.mult))
            step(v.tensor_tensor(caps, caps, tmp, ALU.add))
            if CAP_CUT:
                step(v.tensor_scalar(caps, caps, float(CAP_CUT), None, ALU.subtract))
            step(v.scalar_tensor_tensor(tmp, do, 128.0, so, ALU.mult, ALU.add))
            step(v.tensor_scalar(tmp, tmp, 129.0, None, ALU.add))
            step(v.scalar_tensor_tensor(tmp, t9, 16384.0, tmp, ALU.mult, ALU.add))
            step(v.scalar_tensor_tensor(rec[:, :, 0], t2, 262144.0, tmp, ALU.mult, ALU.add))

            key_c, bid_c, place_c, more_c, caps_c = (a.rearrange("p (c j) -> p c j", j=CT) for a in (key3, bid, place, more, caps))
            sim_c = simv[:, :].rearrange("p (c j) -> p c j", j=CT)
            slot_c = slot[:, :].rearrange("p (c j) -> p c j", j=CT)
            notok_c = notok[:, :].rearrange("p (c j) -> p c j", j=CT)
            rec_c = rec[:, :, 1].rearrange("p (c j) -> p c j", j=CT)

            def one_hot_rows(c):
                v.tensor_tensor(oh[:, :, :], iot[0:B, 0:KEYS].unsqueeze(1).to_broadcast([B, CT, KEYS]),
                                key_c[:, c, :].unsqueeze(2).to_broadcast([B, CT, KEYS]), ALU.is_equal).then_inc(S["oh_ready"], 1)

            one_hot_rows(0)
            for c in range(NCH):
                dve.wait_ge(S[f"attr_in{c % 2}"], 32 * (c // 2 + 1))
                v.tensor_tensor(prod, attr_buf[c % 2], q_n[:, :].unsqueeze(1).to_broadcast([B, CT, D]), ALU.mult)\
                    .then_inc(S["prod_done"], 1)
                dve.wait_ge(S["square_done"], c + 1)
                step(v.tensor_reduce(r_t[:, 6, :], squa, AXX, ALU.add))
                v.tensor_scalar(norm2[:, c % 2, :], r_t[:, 6, :], 1e-24, None, ALU.max).then_inc(S["norm_in"], 1)
                dve.wait_ge(S["prod_done"], c + 1)
                v.tensor_reduce(dots[:, c % 2, :], prod, AXX, ALU.add).then_inc(S["sums_done"], 1)
                step(v.tensor_tensor(lane_eq[:, :, :], bid_c[:, c, :].unsqueeze(1).to_broadcast([B, CT, CT]),
                                     bid_c[:, c, :].unsqueeze(2).to_broadcast([B, CT, CT]), ALU.is_equal))
                step(v.tensor_tensor(lane_eq[:, :, :], lane_eq[:, :, :], earlier[:, :, :], ALU.mult))
                step(v.tensor_reduce(r_t[:, 0, :], lane_eq[:, :, :], AXX, ALU.add))
                dve.wait_ge(S["table_ps0"], 2 * (c + 1))
                win = base_tab[:, WIN[c]:WIN[c] + W3, :].rearrange("p a b -> p (a b)")
                step(v.tensor_tensor(table[:, :], acc[0][0:B, 0:KEYS], win, ALU.add))
                step(v.tensor_tensor(win, win, acc[1][0:B, 0:KEYS], ALU.add))
                step(v.tensor_tensor(found, oh[:, :, :], table[:, :].unsqueeze(1).to_broadcast([B, CT, KEYS]), ALU.mult))
                if c + 1 < NCH:
                    one_hot_rows(c + 1)
                step(v.tensor_reduce(r_t[:, 1, :], found, AXX, ALU.add))
                step(v.tensor_tensor(r_t[:, 2, :], r_t[:, 0, :], r_t[:, 1, :], ALU.add))
                step(v.scalar_tensor_tensor(r_t[:, 3, :], r_t[:, 2, :], float(SLOTS), place_c[:, c, :], ALU.mult, ALU.add))
                step(v.scalar_tensor_tensor(r_t[:, 4, :], r_t[:, 2, :], float(LANES), more_c[:, c, :], ALU.is_ge, ALU.mult))
                step(v.tensor_tensor(r_t[:, 5, :], r_t[:, 3, :], r_t[:, 4, :], ALU.add))
                step(v.tensor_tensor(notok_c[:, c, :], r_t[:, 2, :], caps_c[:, c, :], ALU.is_ge))
                step(v.scalar_tensor_tensor(slot_c[:, c, :], notok_c[:, c, :], FAR, r_t[:, 5, :], ALU.mult, ALU.add))
                dve.wait_ge(S["sums_done"], c + 1)
                dve.wait_ge(S["norm_out"], c + 1)
                step(v.reciprocal(r_t[:, 7, :], normr[:, c % 2, :]))
                step(v.tensor_tensor(sim_c[:, c, :], dots[:, c % 2, :], r_t[:, 7, :], ALU.mult))
                v.tensor_copy(rec_c[:, c, :], sim_c[:, c, :]).then_inc(S["slots_ready"], 1)
            step(v.tensor_reduce(nov[0:B, 0:1], notok[:, :], AXX, ALU.add))
            v.tensor_copy(nov[0:B, 1:2], ones_bf[0:B, 0:1]).then_inc(S["nov_in"], 1)
            dve.wait_ge(S["nov_ps"], 1)
            v.tensor_copy(nov_i[:, :], gx[0:1, 8:9]).then_inc(S["nov_ready"], 1)
            dve.wait_ge(S["wt_used"], 16)
            v.tensor_tensor(nwT[:, :], dn[1][:, 0:D], wtb_s[:, :], ALU.add).then_inc(S["nw_ready"], 1)

            def split(i, xs, g):
                blk = slice(g * GB, (g + 1) * GB)
                hi, mid, lo = (xs3[i][0:B, n, blk, :] for n in range(3))
                step(v.tensor_copy(hi, xs[0:B, blk, :]))
                step(v.tensor_tensor(sp_t, xs[0:B, blk, :], hi, ALU.subtract))
                step(v.tensor_copy(mid, sp_t))
                v.tensor_tensor(lo, sp_t, mid, ALU.subtract).then_inc(S["split_ready"], 1)
                split_n[0] += 1
                dve.wait_ge(S["split_ready"], split_n[0])

            sp_t = sq[:, :, :]
            split_n = [0]
            dve.wait_ge(S["ld_x"], 16)
            for g in range(G):
                split(0, xa, g)
            dve.wait_ge(S["sums_done"], NCH)
            step(v.memset(row_c.rearrange("p r m n -> p (r m n)"), 0.0))
            S_row = v.memset(row_s.rearrange("p r n -> p (r n)"), 0.0)
            S_row.then_inc(S["row_init"], 2)
            dve.wait_ge(S["bucket_in"], 16 * KC)
            dve.wait_ge(S["prefilled"], 16 * KC)
            so_f, do_f, t1_f, hi_f, mid_f, lo_f = (fld[:, n, :] for n in range(6))
            w = [work[:, n * SLOTS:(n + 1) * SLOTS] for n in range(4)]
            step(v.tensor_tensor(w[0], bk[:, 0, :, 0], bk[:, 1, :, 0], ALU.add))
            step(v.tensor_tensor(w[1], bk[:, 0, :, 1], bk[:, 1, :, 1], ALU.add))
            for k in range(2, KC):
                step(v.tensor_tensor(w[0], w[0], bk[:, k, :, 0], ALU.add))
                step(v.tensor_tensor(w[1], w[1], bk[:, k, :, 1], ALU.add))
            rnd = back[:, 3904:3904 + SLOTS // 2].bitcast(BF16)
            step(v.tensor_copy(rnd, w[1]))
            step(v.tensor_copy(hi_f, rnd))
            step(v.tensor_tensor(w[2], w[1], hi_f, ALU.subtract))
            step(v.tensor_copy(rnd, w[2]))
            step(v.tensor_copy(mid_f, rnd))
            step(v.tensor_tensor(lo_f, w[2], mid_f, ALU.subtract))
            step(v.tensor_scalar(t1_f, w[0], 262144.0, None, ALU.is_ge))
            step(v.scalar_tensor_tensor(w[0], t1_f, -262144.0, w[0], ALU.mult, ALU.add))
            floor_div(w[3], w[0], 16384.0, w[1])
            step(v.scalar_tensor_tensor(w[0], w[3], -16384.0, w[0], ALU.mult, ALU.add))
            floor_div(w[2], w[0], 128.0, w[1])
            step(v.scalar_tensor_tensor(w[0], w[2], -128.0, w[0], ALU.mult, ALU.add))
            step(v.tensor_scalar(so_f, w[0], 1.0, None, ALU.subtract))
            step(v.tensor_scalar(do_f, w[2], 1.0, None, ALU.subtract))
            step(v.tensor_scalar(featc[:, :, 0], t1_f, 0.0, None, ALU.is_equal))
            step(v.tensor_copy(featc[:, :, 1], t1_f))
            step(v.memset(featc[:, :, 2], 1.0))
            step(v.tensor_tensor(featc[:, :, 3:12], w[3].unsqueeze(2).to_broadcast([128, SLOTS, 9]),
                                 iot[:, 0:9].unsqueeze(1).to_broadcast([128, SLOTS, 9]), ALU.is_equal))

            def one_hots(piece, diagonal, before_n):
                v.tensor_scalar(fb[:, :, 0:25], fld[:, :, bass.ds(25 * piece, 25)], 1.0, None, ALU.mult).then_inc(S["fields_ready"], 1)
                if diagonal:
                    g5 = 20 if isinstance(piece, int) else piece // 6 * 5
                    v.tensor_scalar(fb[:, :, 25:30], fld[:, :, bass.ds(625 + g5, GB)], 1.0, None, ALU.mult).then_inc(S["fields_ready"], 1)
                    dve.wait_ge(S["fields_ready"], DIAG_F(piece))
                else:
                    dve.wait_ge(S["fields_ready"], OFF_F(piece))
                for r in range(GB):
                    for tiles in row_order(r, diagonal):
                        for n, col in tiles:
                            o = n % OHR
                            dve.wait_ge(S["oh_used"], before_n + n + 1)
                            v.tensor_scalar(ohs[:, o, 0:B], iota_bf[:, 0:B], fb[:, 0, col:col + 1], None, ALU.is_equal)
                            v.tensor_scalar(ohd[:, o, 0, :], iota_bf[:, 0:B], fb[:, 1, col:col + 1], None, ALU.is_equal)
                            for m in range(1, 5):
                                last = v.tensor_scalar(ohd[:, o, m, :], iota_bf[:, 0:B], fb[:, 1, col:col + 1],
                                                       fb[:, 1 + m, col:col + 1], ALU.is_equal, ALU.mult)
                            last.then_inc(S["oh_full"], 1)
                dve.wait_ge(S["oh_full"], before_n + (30 if diagonal else 25))
                v.memset(mark2[:, :], 0.0)

            def DIAG_F(piece):
                return piece + (piece // 6 if isinstance(piece, int) else piece // 6) + 2

            def OFF_F(piece):
                return piece + (piece - 1) // 6 + 2

            piece_loop(dve, one_hots)

            dve.wait_ge(S["nov_ready"], 1)
            over_n = dve.value_load(nov_i[0:1, 0:1], min_val=0, max_val=E)
            with dve.If(over_n > 0):
                fb_step = Steps(dve, S["fbv"])
                fb_step(v.tensor_scalar(key, key, 1.0, None, ALU.add))
                fb_step(v.tensor_tensor(key, key, notok[:, :], ALU.mult))
                fb_step(v.tensor_scalar(key, key, 1.0, None, ALU.subtract))
                dve.wait_ge(S["tile_done"], 1)
                with dve.Fori(0, T) as t:
                    n_ = [0]

                    def lk(ins):
                        n_[0] += 1
                        ins.then_inc(S["fbv"], 1)
                        dve.wait_ge(S["fbv"], 3 + 13 * t + n_[0])

                    at = bass.ds(t, 1)
                    v.tensor_copy(kcol[:, 0:1], key[:, at])
                    v.tensor_copy(kcol[:, 1:2], notok[:, at])
                    v.tensor_scalar(ohoff[:, :], iota_bf[0:B, 0:B], do[:, at], None, ALU.is_equal)
                    v.tensor_copy(frow[:, 1:2], t2[:, at])
                    lk(v.tensor_scalar(frow[:, 3:12], iot[0:B, 0:9], t9[:, at], None, ALU.is_equal))
                    v.tensor_scalar(frow[:, 0:1], frow[:, 1:2], 0.0, None, ALU.is_equal)
                    lk(v.memset(frow[:, 2:3], 1.0))
                    v.tensor_copy(v3[:, 0:1], kcol[:, 1:2])
                    v.tensor_tensor(v3[:, 1:2], kcol[:, 1:2], frow[:, 1:2], ALU.mult)
                    v.tensor_tensor(v3[:, 2:3], kcol[:, 1:2], simv[:, at], ALU.mult)
                    lk(v.tensor_scalar(ohdb[:, :], iot[0:B, 0:NB], db[:, at], kcol[:, 1:2], ALU.is_equal, ALU.mult))
                    lk(v.tensor_tensor(rhs12[:, :, :], ohdb[:, :].unsqueeze(2).to_broadcast([B, NB, F]),
                                       frow[:, :].unsqueeze(1).to_broadcast([B, NB, F]), ALU.mult))
                    v.tensor_scalar(kb[:, :], key[:, at].to_broadcast([B, B]), 1.0, None, ALU.mult).then_inc(S["tile_ready"], 1)
                    dve.wait_ge(S["keyrow"], t + 1)
                    lk(v.tensor_scalar(same[:, :], tp[0][0:B, 0:B], kcol[:, 0:1], None, ALU.is_equal))
                    v.tensor_tensor(same_tri[:, :], same[:, :], tri[0:B, 0:B], ALU.mult).then_inc(S["same_ready"], 1)
                    dve.wait_ge(S["same_ready"], t + 1)
                    lk(v.tensor_reduce(rank1[:, :], same_tri[:, :], AXX, ALU.add))
                    lk(v.tensor_scalar(kcol[:, 2:3], kcol[:, 0:1], 0.0, None, ALU.is_lt))
                    lk(v.tensor_tensor(kcol[:, 2:3], kcol[:, 2:3], rank1[:, :], ALU.add))
                    lk(v.tensor_scalar(kcol[:, 2:3], kcol[:, 2:3], 1.0, None, ALU.min))
                    lk(v.scalar_tensor_tensor(kcol[:, 3:4], kcol[:, 0:1], -1.0, lane[0:B], ALU.mult, ALU.add))
                    lk(v.tensor_scalar(kcol[:, 3:4], kcol[:, 3:4], float(ELEMS), None, ALU.add))
                    lk(v.tensor_tensor(kcol[:, 3:4], kcol[:, 3:4], kcol[:, 2:3], ALU.mult))
                    lk(v.tensor_tensor(idx[:, :], kcol[:, 3:4], kcol[:, 0:1], ALU.add))
                    assert n_[0] == 13
                    dve.wait_ge(S["tile_sums"], t + 1)
                    v.tensor_copy(s3[:, :], tp[1][0:B, 0:3]).then_inc(S["idx_ready"], 1)
                    dve.wait_ge(S["tile_done"], t + 2)
                    for m in range(3):
                        dve.wait_ge(oscat[m], 16 * (t + 1))
            dve.wait_ge(S["counts_psum"], 1)
            v.tensor_copy(counts[:, :, 0:F], cnt[0:B, 0:NB * F].rearrange("p (b f) -> p b f", f=F)).then_inc(S["counts_sb"], 1)
            dve.wait_ge(S["counts_sb"], 1)
            step(v.tensor_scalar(halfdeg[:, :], counts[:, :, 2], 1.0, None, ALU.max))
            step(v.reciprocal(halfdeg[:, :], halfdeg[:, :]))
            step(v.tensor_scalar(halfdeg[:, :], halfdeg[:, :], 0.5, None, ALU.mult))

            def layernorm(k, g, xo):
                step(v.tensor_reduce(st[:, 0, :], y[:, :, :], AXX, ALU.add))
                step(v.tensor_scalar(st[:, 0, :], st[:, 0, :], 1.0 / D, None, ALU.mult))
                v.tensor_tensor(yc[:, :, :], y[:, :, :], st[:, 0, :].unsqueeze(2).to_broadcast([B, GB, D]), ALU.subtract)\
                    .then_inc(S["xc_ready"], 1)
                dve.wait_ge(S["sq_ready"], k * G + g + 1)
                v.tensor_reduce(st[:, 1, :], sq[:, :, :], AXX, ALU.add).then_inc(S["sd_in"], 1)
                dve.wait_ge(S["sd_ready"], k * G + g + 1)
                step(v.reciprocal(st[:, 3, :], st[:, 2, :]))
                v.tensor_tensor(xo[0:B, g * GB:(g + 1) * GB, :], yc[:, :, :], st[:, 3, :].unsqueeze(2).to_broadcast([B, GB, D]),
                                ALU.mult).then_inc(S["x_ready"], 1)
                dve.wait_ge(S["x_ready"], k * G + g + 1)

            def relu_add(k, g, xs):
                dve.wait_ge(S["lin_ready"], k * G + g + 1)
                v.scalar_tensor_tensor(y[:, 0:4, :], dn[0][0:B, :].rearrange("p (b d) -> p b d", d=D), 0.0,
                                       xs[0:B, g * GB:g * GB + 4, :], ALU.max, ALU.add)
                v.scalar_tensor_tensor(y[:, 4, :], dn[1][0:B, 0:D], 0.0, xs[0:B, g * GB + 4, :], ALU.max, ALU.add)\
                    .then_inc(S["lin_free"], 1)
                dve.wait_ge(S["lin_free"], k * G + g + 1)

            for g in range(G):
                dve.wait_ge(S["acc_free"], 2 * (L0 * G + g + 1))
                dve.wait_ge(S["t_free"], 7)
                v.tensor_tensor(hT[:, :], agg[:, :], xT[:, g * GW:(g + 1) * GW], ALU.add).then_inc(S["h_ready"], 1)
                dve.wait_ge(S["h_ready"], g + 1)
                dve.sem_inc(S["agg_used"], 1)
                relu_add(0, g, xa)
                layernorm(0, g, xb)
                split(1, xb, g)
            for g in range(G):
                dve.wait_ge(S["acc_free"], 2 * (L1B * G + g + 1))
                dve.wait_ge(S["t_free"], 14)
                v.tensor_tensor(hT[:, :], cT[:, g * GW:(g + 1) * GW], agg[:, :], ALU.subtract).then_inc(S["h_ready"], 1)
                relu_add(1, g, xb)
                dve.sem_inc(S["agg_used"], 1)
                layernorm(1, g, xc)

            def mix(n, g, xs, to):
                dve.wait_ge(S["tr_ready"], (n - L2A) * G + g + 1)
                hd = halfdeg[:, g * GB:(g + 1) * GB].unsqueeze(2)
                v.tensor_tensor(yc[:, 0:4, :], dn[0][0:B, :].rearrange("p (b d) -> p b d", d=D),
                                hd[:, 0:4, :].to_broadcast([B, 4, D]), ALU.mult)
                v.tensor_tensor(yc[:, 4:5, :], dn[1][0:B, 0:D].unsqueeze(1), hd[:, 4:5, :].to_broadcast([B, 1, D]), ALU.mult)\
                    .then_inc(S["tr_free"], 1)
                dve.wait_ge(S["tr_free"], (n - L2A) * G + g + 1)
                dve.sem_inc(S["agg_used"], 1)
                step(v.scalar_tensor_tensor(to, xs[0:B, g * GB:(g + 1) * GB, :], 0.5, yc[:, :, :], ALU.mult, ALU.add))

            for g in range(G):
                mix(L2A, g, xc, xa[0:B, g * GB:(g + 1) * GB, :])
                dve.sem_inc(S["x2_ready"], 1)
            for g in range(G):
                mix(L2B, g, xa, y[:, :, :])
                step(v.tensor_tensor(y[:, :, :], y[:, :, :], xc[0:B, g * GB:(g + 1) * GB, :], ALU.add))
                layernorm(2, g, xb)
                split(0, xb, g)
            for g in range(G):
                for h in range(2):
                    w, lo = HALF[h], h * HALF[0]
                    r, z, n_, t_ = (gr[:, k, lo:lo + w] for k in range(4))
                    xx = xT[:, g * GW + lo:g * GW + lo + w]
                    yy = hT[:, lo:lo + w]
                    dve.wait_ge(S["gates_ready"], 2 * g + h + 1)
                    dve.wait_ge(S["rz_ready"], 2 * (2 * g + h + 1))
                    step(v.scalar_tensor_tensor(t_, cnt[:, 0:w], b3[:, 1, 2:3], r, ALU.add, ALU.mult))
                    v.tensor_tensor(t_, t_, gx[:, 0:w], ALU.add).then_inc(S["n_in"], 1)
                    dve.wait_ge(S["n_ready"], 2 * g + h + 1)
                    if g and not h:
                        dve.wait_ge(S["yt_ready"], g)
                    step(v.tensor_tensor(yy, xx, n_, ALU.subtract))
                    step(v.tensor_tensor(yy, yy, z, ALU.mult))
                    step(v.tensor_tensor(yy, yy, n_, ALU.add))
                    v.tensor_tensor(yy, yy, xx, ALU.add).then_inc(S["yT_ready"], 1)
                dve.wait_ge(S["msg_ready"], 2 * (g + 1))
                dve.sem_inc(S["agg_used"], 1)
                dve.wait_ge(S["y_ready"], 2 * (g + 1))
                layernorm(3, g, xa)



_INS = ['x', 'src', 'dst', 'edge_attr_128', 'edge_type_2', 'edge_type_9', 'L0_gnn_memory', 'L0_gnn_gru_w_ih',
        'L0_gnn_gru_b_ih', 'L0_gnn_gru_b_hh', 'L0_gnn_wt_w', 'L0_gnn_wt_b', 'L0_gnn_lin_b', 'L1_gnn_W_data',
        'L1_gnn_b_data', 'L1_gnn_W_control', 'L1_gnn_b_control', 'L1_gnn_W_self', 'L1_gnn_b_self',
        'L2_gnn_question_emb', 'L3_gnn_W_msg', 'L3_gnn_b_msg', 'L3_gnn_edge_embed', 'L3_gnn_W_ih', 'L3_gnn_W_hh',
        'L3_gnn_b_ih', 'L3_gnn_b_hh']


def kernel(**inputs):
    import numpy as _np
    import concourse.bacc as _bacc
    from concourse import mybir as _mybir
    from concourse.bass_utils import run_bass_kernel_spmd as _run

    def lay(name, a):
        if name == 'L0_gnn_wt_b':
            return a.reshape(D, D).T
        if 'gru_b' in name or name in ('L3_gnn_b_ih', 'L3_gnn_b_hh'):
            return a.reshape(3, D).T
        if '_W_' in name or '_w_ih' in name or name in ('L0_gnn_memory', 'L0_gnn_wt_w'):
            return a.T
        return a

    nc = _bacc.Bacc("TRN2", target_bir_lowering=False, num_devices=1)
    arrays, args = {}, []
    for name in _INS:
        a = _np.ascontiguousarray(lay(name, _np.asarray(inputs[name])))
        arrays[f"in_{name}"] = a
        args.append(nc.dram_tensor(f"in_{name}", a.shape, _mybir.dt.from_np(a.dtype), kind="ExternalInput").ap())
    args.append(nc.dram_tensor("out_0", (N, D), _mybir.dt.float32, kind="ExternalOutput").ap())
    program(nc, *args)
    r = _run(nc, [arrays], core_ids=[0])
    return r.results[0]["out_0"]
```

```python
from contextlib import ExitStack

import concourse.bass as bass
from concourse import mybir

ALU = mybir.AluOpType
ACT = mybir.ActivationFunctionType
F32 = mybir.dt.float32
BF16 = mybir.dt.bfloat16
I32 = mybir.dt.int32
AXX = mybir.AxisListType.X

D = 128
N = 3125
E = 53125
B = 125
NB = N // B
G = 5
GB = NB // G
GW = GB * B
HALF = (313, 312)
T = E // B
CT = 25
NCH = T // CT
PIECE = GB * GW
ROW = 3136
NPIECE = G * G
W3 = 3
WIN = [(25 * c + 13) // 17 for c in range(NCH)]
KEYS = W3 * NB
SLOTS = NB * NB + NB
LANES = 128
GC = NB * GB + GB
LG = 3
EARLY = next(c for c in range(NCH) if WIN[c] - 1 >= LG * GB)
LATE_AT = LG * GC
LATE = SLOTS - LATE_AT
ATONCE = 22
KC, KL = 5, 4
RING = 4
ELEMS = NPIECE * 128 * ROW
F = 12
FN = F + 1
EPS = 1e-5
MAGIC = 12582912.0
FAR = 16777216.0


class Steps:

    def __init__(self, eng, sem):
        self.eng, self.sem, self.n = eng, sem, 0

    def __call__(self, ins):
        self.n += 1
        ins.then_inc(self.sem, 1)
        self.eng.wait_ge(self.sem, self.n)


def program(nc, x, src, dst, attr, ty2, ty9, mem, wih0, bih0, bhh0, wt, wtb, linb,
            wd, bd, wc, bc, ws, bs, quest, wmsg, bmsg, embed, wih, whh, bih, bhh, out):
    with ExitStack() as ctx:
        def sb(name, shape, dt=F32):
            return ctx.enter_context(nc.sbuf_tensor(name, shape, dt))

        def pb(name):
            return ctx.enter_context(nc.psum_tensor(name, [128, 512], F32))

        def sem(name):
            return ctx.enter_context(nc.semaphore(name))

        COUNT, CTRL, SIM = 0, 1, 2
        dts = [BF16, BF16, F32]
        dense = [nc.dram_tensor(n, [ELEMS + 128, 1], dt, kind="Internal").ap()
                 for n, dt in zip(("count_all", "count_ctrl", "sim_sum"), dts)]
        over = [nc.dram_tensor(n, [ELEMS + 128, 1], F32, kind="Internal").ap() for n in ("over_all", "over_ctrl")]

        def pieces(a):
            return a[0:ELEMS, :].rearrange("(q p n) o -> q p (n o)", p=128, n=ROW)

        dense_v = [pieces(a) for a in dense]
        over_v = [pieces(a) for a in over]
        over_dst = [over[0], over[1], dense[SIM]]
        buckets = [nc.dram_tensor(f"bucket{k}", [LANES * SLOTS, 2], F32, kind="Internal").ap() for k in range(KC)]
        late = [nc.dram_tensor(f"late{k}", [LANES * SLOTS, 2], F32, kind="Internal").ap() for k in range(KL)]

        ring = sb("ring", [128, RING, 3200])
        xa = sb("xa", [128, NB, D])
        xb = sb("xb", [128, NB, D])
        xc = sb("xc", [128, NB, D])
        xT = sb("xT", [D, N])
        cT = sb("cT", [D, N])
        wtr = xT[:, 0:2048].rearrange("p (a n) -> p a n", a=2)
        xs3 = [sb(f"xs3_{i}", [128, 3, NB, D], BF16) for i in range(2)]
        obuf = sb("obuf", [128, GW])
        work = sb("work", [128, GB * GW + 64])

        def part(at, shape, dt=F32, lanes=B):
            n = 1
            for d in shape:
                n *= d
            words = n if dt == F32 else (n + 1) // 2
            a = work[0:lanes, at:at + words]
            if dt != F32:
                a = a.bitcast(dt)[:, 0:n]
            if len(shape) == 2:
                a = a.rearrange("p (a b) -> p a b", b=shape[1])
            return a

        ei = xb[0:B, :, :].rearrange("p b d -> p (b d)").bitcast(I32)[:, 0:4 * T].rearrange("p (n t) -> p n t", t=T)
        xbf = xb[0:B, :, :].rearrange("p b d -> p (b d)")
        xcf = xc[0:B, :, :].rearrange("p b d -> p (b d)")
        ef = [cT[0:B, n * T:(n + 1) * T] for n in range(7)] + [xcf[:, n * T:(n + 1) * T] for n in range(7)]
        efx = [xbf[:, n * T:(n + 1) * T] for n in range(4, 7)]
        rec = sb("rec", [B, T, 2])
        simv = sb("simv", [B, T])
        slot = sb("slot", [B, T], I32)
        notok = sb("notok", [B, T])
        ssq = sb("ssq", [B, 2, CT])
        norm2 = sb("norm2", [B, 2, CT])
        normr = sb("normr", [B, 2, CT])
        dots = sb("dots", [B, 2, CT])
        iot_i = sb("iot_i", [128, 257], I32)
        iot = sb("iot", [128, 257])
        ident = sb("ident", [128, 128])
        tri = sb("tri", [128, 128])
        before = sb("before", [B, B], BF16)
        ones_bf = sb("ones_bf", [128, 128], BF16)
        iota_bf = sb("iota_bf", [128, 256], BF16)
        zrow = sb("zrow", [128, 512], BF16)
        q_bc = sb("q_bc", [B, D])
        q_n = sb("q_n", [B, D])
        q_s = sb("q_s", [B, 4])
        winoff = sb("winoff", [B, 3, NCH])
        oh = part(0, [CT, KEYS], BF16)
        lane_eq = part(940, [CT, CT])
        earlier = part(1565, [CT, CT])
        base_tab = part(2190, [NB + 2, NB])
        table = part(2865, [KEYS])
        found = xs3[0][0:B, :, :, :].rearrange("p a b d -> p (a b d)").bitcast(F32)[:, 0:CT * KEYS].rearrange("p (j b) -> p j b", b=KEYS)
        r_t = part(2940, [8, CT])
        nov = sb("nov", [128, 4])
        nov_i = sb("nov_i", [1, 1], I32)
        fb = sb("fb", [128, 4, 30])
        kb = sb("kb", [B, B])
        kcol = sb("kcol", [B, 4])
        v3 = sb("v3", [B, 3])
        s3 = sb("s3", [B, 3])
        same = sb("same", [B, B])
        same_tri = sb("same_tri", [B, B])
        rank1 = sb("rank1", [B, 1])
        idx = sb("idx", [B, 1], I32)
        ohoff = sb("ohoff", [B, B], BF16)
        ohdb = sb("ohdb", [B, NB])
        frow = sb("frow", [B, F])
        rhs12 = sb("rhs12", [B, NB, F], BF16)
        counts = sb("counts", [B, NB, FN])
        countsT = sb("countsT", [FN, N])
        halfdeg = sb("halfdeg", [B, NB])
        r0 = sb("r0", [FN, D])
        r1 = sb("r1", [FN, D])
        r3 = sb("r3", [FN, D])
        mem_c = sb("mem_c", [D, 1])
        wih0_s = sb("wih0_s", [D, 3 * D])
        b0 = sb("b0", [D, 2, 3])
        gru = sb("gru", [D, 10])
        wtb_s = sb("wtb_s", [D, D])
        nwT = sb("nwT", [D, D])
        w1 = sb("w1", [D, 3, D])
        wmsg_s = sb("wmsg_s", [D, D])
        wih_s = sb("wih_s", [D, 3 * D])
        whh_s = sb("whh_s", [D, 3 * D])
        b3 = sb("b3", [D, 2, 3])
        b3s = sb("b3s", [D, 3])
        agg = part(0, [GW], lanes=D)
        hT = part(GW, [GW], lanes=D)
        mT = cT[:, 4 * GW:5 * GW]
        gr = cT[:, 0:4 * GW].rearrange("p (n w) -> p n w", w=GW)
        y, yc, sq = (part(2 * GW + n * GB * D, [GB, D]) for n in range(3))
        st = sb("st", [B, 4, GB])
        epsc = sb("epsc", [128, 1])
        mark = sb("mark", [1, 1])
        mark2 = sb("mark2", [1, 1])

        row_c = ring[:, 0, 0:GB * GW].bitcast(BF16).rearrange("p (r m n) -> p r m n", r=GB, m=2)
        row_s = ring[:, 1, 0:GB * GW].rearrange("p (r n) -> p r n", r=GB)
        back = ring[:, 2:4, :].rearrange("p a n -> p (a n)")
        places = [work[:, :], xb[:, :, :].rearrange("p b d -> p (b d)"), xT[:, :]]
        ohs = [a[:, 0:384].bitcast(BF16).rearrange("p (t n) -> p t n", n=128) for a in places]
        ohs_f = [a[:, 384:1152].rearrange("p (t n) -> p t n", n=128) for a in places]
        ohd = [a[:, 1152:1920].bitcast(BF16).rearrange("p (t m n) -> p t m n", m=2, n=128) for a in places]
        ohsim = [a[:, 1920:2688].rearrange("p (t n) -> p t n", n=128) for a in places]
        late_w = [back[:, 3904 + n * LATE:3904 + (n + 1) * LATE] for n in range(4)]
        early_sum = [obuf[:, n * LATE:(n + 1) * LATE] for n in range(2)]
        featc = back.bitcast(BF16)[:, 0:SLOTS * F].rearrange("p (s f) -> p s f", f=F)
        fields = xs3[1][:, :, :, :].rearrange("p a b d -> p (a b d)").bitcast(F32)
        fld = fields[:, 0:5 * SLOTS].rearrange("p (n s) -> p n s", s=SLOTS)
        bk = [a[:, 0:2 * SLOTS].rearrange("p (s e) -> p s e", e=2)
              for a in [back[:, 2 * SLOTS * k:] for k in range(KC - 1)] + [fields[:, 5 * SLOTS:]]]
        late_in = [a[:, n * 2 * LATE:(n + 1) * 2 * LATE].rearrange("p (s e) -> p s e", e=2)
                   for a in (back[:, (KC - 1) * SLOTS * 2:], fields[:, 5 * SLOTS:]) for n in range(2)]
        zero = fields[:, 0:2 * SLOTS]

        bank_sets = [ctx.enter_context(nc.psum_tensor(f"banks{i}", [128, 3, 512], F32)) for i in range(2)]
        acc = [bank_sets[0][:, 0, :], bank_sets[0][:, 1, :]]
        dn = [bank_sets[0][:, 2, :], bank_sets[1][:, 0, :]]
        tp = [bank_sets[1][:, 1, :], bank_sets[1][:, 2, :]]
        flat = [a[0:B, :, :].rearrange("p a n -> p (a n)") for a in bank_sets]
        ps_c = [a[:, 12:12 + 6 * B].rearrange("p (c m n) -> p c m n", m=2, n=B) for a in flat]
        ps_s = [a[:, 1024:1024 + 3 * B].rearrange("p (c n) -> p c n", n=B) for a in flat]
        cnt = pb("cnt")
        gx = pb("gx")

        names = """ld_edges ld_x ld_w ld_q zeroed iota_done consts prod_done square_done sums_done norm_in norm_out attr_in0
            attr_in1 oh_ready table_ps0 slots_ready prefilled bucket_in late_back nov_in nov_ps nov_ready
            fields_ready row_init ohs_ready ohs_f_ready oh_full oh_used group_ps rows_ready built tile_ready keyrow
            same_ready tile_sums idx_ready tile_done over_zero over_zero_b over_in over_used fbv counts_ps
            counts_free counts_psum counts_sb q_ssq q_norm q_ready gi gru_ready0 gru_rz gru_t gru_n u_ready wt_in0
            wt_in1 wt_used nw_ready w_small acc_free h_ready lin_ready lin_free xc_ready sq_ready sd_in sd_ready
            x_ready split_ready t_ready t_free tr_ready tr_free msg_ready m_ready gates_ready rz_ready n_in n_ready
            yT_ready yt_ready y_ready out_done piece_used dve agg_used x2_ready""".split()
        S = {n: sem(n) for n in names}
        piece_in = [sem(f"piece_in{k}") for k in range(RING)]
        scat = [sem(f"scat{k}") for k in range(KC)]
        late_scat = [sem(f"late_scat{k}") for k in range(KL)]
        oscat = [sem(f"oscat{k}") for k in range(3)]
        row_out = [sem(f"row_out{r}") for r in range(GB)]

        attr_v = attr.rearrange("(c p j) d -> c p j d", p=B, j=CT)
        attr_buf = [ring[0:B, i, :].rearrange("p (t d) -> p t d", d=D) for i in range(2)]
        prod = ring[0:B, 2, :].rearrange("p (t d) -> p t d", d=D)
        squa = ring[0:B, 3, :].rearrange("p (t d) -> p t d", d=D)
        L0, L1A, L1B, L2A, L2B, L3 = range(6)
        PASSES = [(COUNT, xs3[0]), (COUNT, xs3[1]), (CTRL, xs3[1]), (SIM, xc), (SIM, xa), (COUNT, xs3[0])]

        CPASS = {L0: 0, L1A: 1, L1B: 2, L3: 3}

        block = ctx.enter_context(nc.Block())

        def piece_loop(eng, body, at_end=None, groups=(0, G)):
            with eng.Fori(*groups) as g:
                body(G * g, (G + 1) * g, g, True)
                with eng.Fori(1, G) as i:
                    k = nc.s_assert_within(g + i - G * (((g + i) * 13) >> 6), 0, G - 1,
                                           skip_runtime_bounds_check_because="it is g + i modulo 5, for g + i up to 8")
                    body(G * g + i, G * g + k, g, False)
                if at_end:
                    at_end(g)

        def place_of(r):
            return r % 3, (2, 2, 5, 3, 3)[r]

        def tiles_of(r, c, diagonal):
            return [c] + ([GB] if diagonal and c == r else [])

        @block.sync
        def _(sp):
            for n, a in enumerate((dst, src, ty2, ty9)):
                sp.dma_start(ei[:, n, :].rearrange("p (c j) -> p c j", j=CT), a.rearrange("(c p j) -> p c j", p=B, j=CT))\
                    .then_inc(S["ld_edges"], 16)
            sp.dma_start(q_bc[:, :], quest.partition_broadcast(B).rearrange("p a d -> p (a d)")).then_inc(S["ld_q"], 16)
            sp.wait_ge(S["zeroed"], 1)
            for k in range(KC):
                sp.dma_start(buckets[k].rearrange("(p s) e -> p (s e)", p=LANES), zero).then_inc(S["prefilled"], 16)
            for k in range(KL):
                sp.dma_start(late[k].rearrange("(p s) e -> p (s e)", p=LANES)[:, 2 * LATE_AT:2 * SLOTS], zero[:, 0:2 * LATE])\
                    .then_inc(S["prefilled"], 16)
            for c in range(NCH):
                if c >= 2:
                    sp.wait_ge(S["prod_done"], c - 1)
                    sp.wait_ge(S["square_done"], c - 1)
                for lo, hi in ((0, 112), (112, B)):
                    sp.dma_start(attr_buf[c % 2][lo:hi], attr_v[c, lo:hi]).then_inc(S[f"attr_in{c % 2}"], 16)
                if c == 1:
                    sp.dma_start(xa[0:B, :, :], x.rearrange("(b p) d -> p b d", p=B)).then_inc(S["ld_x"], 16)
            sp.wait_ge(S["sums_done"], NCH)
            for k in range(KC):
                sp.wait_ge(scat[k], 16 * len(range(k, EARLY * CT, KC)))
                sp.dma_start(bk[k], buckets[k].rearrange("(p s) e -> p s e", p=LANES)).then_inc(S["bucket_in"], 16)

            def rows(n, piece, g, diagonal):
                for r in range(GB):
                    sp.wait_ge(S["rows_ready"], 4 * (GB * n + r + 1) + 4)
                    for m in range(2):
                        sp.dma_start(dense_v[m][bass.ds(piece, 1), :, r * GW:(r + 1) * GW].rearrange("a p n -> (a p) n"),
                                     row_c[:, r, m, :]).then_inc(row_out[r], 16)
                    sp.dma_start(dense_v[SIM][bass.ds(piece, 1), :, r * GW:(r + 1) * GW].rearrange("a p n -> (a p) n"),
                                 row_s[:, r, :]).then_inc(row_out[r], 16)

            piece_loop(sp, rows)
            for r in range(GB):
                sp.wait_ge(row_out[r], 48 * (NPIECE + 1))
            sp.sem_inc(S["built"], 1)
            sp.wait_ge(S["nov_ready"], 1)
            over_n = sp.value_load(nov_i[0:1, 0:1], min_val=0, max_val=E)
            with sp.If(over_n > 0):
                sp.wait_ge(S["over_zero"], 1)
                for m in range(2):
                    for q in range(NPIECE):
                        for r in range(GB):
                            sp.dma_start(over_v[m][q][:, r * GW:(r + 1) * GW], obuf[:, :]).then_inc(S["over_zero_b"], 16)
                for m in range(3):
                    sp.wait_ge(oscat[m], 16 * T)
            for n, (m, _) in enumerate(PASSES):
                for g in range(G):
                    for k in range(G):
                        if m != SIM and k == G - 1:
                            with sp.If(over_n > 0):
                                for s in range(NB):
                                    at = (CPASS[n] * G + g) * NB + s
                                    if at:
                                        sp.wait_ge(S["over_used"], at)
                                    q, r = divmod(s, GB)
                                    sp.dma_start(obuf[:, :], over_v[m][g * G + q][:, r * GW:(r + 1) * GW])\
                                        .then_inc(S["over_in"], 16)
                        at = (n * G + g) * G + k
                        if at >= RING:
                            sp.wait_ge(S["piece_used"], at - RING + 1)
                        elif at == 2:
                            sp.wait_ge(S["counts_psum"], 1)
                        to = ring[:, at % RING, 0:PIECE] if m == SIM else ring[:, at % RING, 0:ROW // 2].bitcast(BF16)[:, 0:PIECE]
                        sp.dma_start(to, dense_v[m][g * G + k][:, 0:PIECE]).then_inc(piece_in[at % RING], 16)
            out_v = out.rearrange("(b p) d -> p b d", p=B)
            for g in range(G):
                sp.wait_ge(S["x_ready"], 3 * G + g + 1)
                sp.dma_start(out_v[:, g * GB:(g + 1) * GB, :], xa[0:B, g * GB:(g + 1) * GB, :]).then_inc(S["out_done"], 16)
            sp.wait_ge(S["out_done"], 16 * G)

        @block.gpsimd
        def _(pool):
            nc.gpsimd.iota(iot_i[:, 0:256], pattern=[[1, 256]], base=0, channel_multiplier=0).then_inc(S["iota_done"], 1)
            nc.gpsimd.iota(iot_i[:, 256:257], pattern=[[1, 1]], base=0, channel_multiplier=1).then_inc(S["iota_done"], 1)
            nc.gpsimd.memset(zero, 0.0).then_inc(S["zeroed"], 1)
            pool.wait_ge(S["prefilled"], 16 * (KC + KL))

            def scatter(t):
                if t % CT == 0:
                    pool.wait_ge(S["slots_ready"], t // CT + 1)
                if t < EARLY * CT:
                    k, turn, to, landed = t % KC, t // KC, buckets, scat
                else:
                    k, turn, to, landed = (t - EARLY * CT) % KL, (t - EARLY * CT) // KL, late, late_scat
                if turn:
                    pool.wait_ge(landed[k], 16 * turn)
                nc.gpsimd.indirect_dma_start(
                    to[k], bass.IndirectOffsetOnAxis(ap=slot[:, t:t + 1], axis=0), rec[:, t, :], None,
                    bounds_check=LANES * SLOTS - 1, oob_is_err=False).then_inc(landed[k], 16)

            for t in range(EARLY * CT + ATONCE):
                scatter(t)

            def widen_row(n, r, diagonal):
                o = ohs[place_of(r)[0]][:, 0:GB + diagonal, 0:B]
                pool.wait_ge(S["ohs_ready"], GB * n + r + 1)
                nc.gpsimd.tensor_tensor(ohs_f[place_of(r)[0]][:, 0:GB + diagonal, 0:B], o, o, ALU.mult)\
                    .then_inc(S["ohs_f_ready"], 1)

            def widen(n, piece, g, diagonal):
                for r in range(GB):
                    widen_row(n, r, diagonal)

            at, rest, shared = EARLY * CT + ATONCE, T - EARLY * CT - ATONCE, LG * G * GB - 8
            for i in range(LG * G * GB):
                if i == shared:
                    for k in range(KL):
                        pool.wait_ge(late_scat[k], 16 * len(range(k, T - EARLY * CT, KL)))
                        nc.gpsimd.dma_start(late_in[k], late[k].rearrange("(p s) e -> p s e", p=LANES)[:, LATE_AT:SLOTS, :])\
                            .then_inc(S["late_back"], 16)
                widen_row(i // GB, i % GB, i % (G * GB) < GB)
                if i < shared:
                    for t in range(at + i * rest // shared, at + (i + 1) * rest // shared):
                        scatter(t)
            piece_loop(pool, widen, groups=(LG, G))
            pool.wait_ge(S["nov_ready"], 1)
            over_n = pool.value_load(nov_i[0:1, 0:1], min_val=0, max_val=E)
            with pool.If(over_n > 0):
                pool.wait_ge(S["built"], 1)
                nc.gpsimd.memset(obuf[:, :], 0.0).then_inc(S["over_zero"], 1)
                pool.wait_ge(S["over_zero_b"], 16 * 2 * NPIECE * GB)
                nc.gpsimd.memset(mark[:, :], 0.0).then_inc(S["tile_done"], 1)
                last_elem = pool.to_reg(ELEMS + 127)
                with pool.Fori(0, T) as t:
                    pool.wait_ge(S["idx_ready"], t + 1)
                    nc.gpsimd.tensor_tensor(mark[:, :], kcol[0:1, 0:1], kcol[0:1, 0:1], ALU.add)\
                        .then_inc(S["tile_done"], 1)
                    for m in range(3):
                        nc.gpsimd.indirect_dma_start(
                            over_dst[m], bass.IndirectOffsetOnAxis(ap=idx[:, 0:1], axis=0), s3[:, m:m + 1], None,
                            bounds_check=last_elem, oob_is_err=True, compute_op=ALU.add).then_inc(oscat[m], 16)

        @block.scalar
        def _(act):
            small = [(mem_c[:, :], mem), (wih0_s[:, :], wih0), (b0[:, 0, :], bih0), (b0[:, 1, :], bhh0), (wtb_s[:, :], wtb),
                     (w1[:, 0, :], wd), (w1[:, 1, :], wc), (w1[:, 2, :], ws), (wmsg_s[:, :], wmsg), (wih_s[:, :], wih),
                     (whh_s[:, :], whh), (b3[:, 0, :], bih), (b3[:, 1, :], bhh)]
            for o, i in small:
                act.dma_start(o, i).then_inc(S["ld_w"], 16)
            act.wait_ge(S["w_small"], 1)
            for o, i in ((r0[12:13, :], linb), (r1[0:1, :], bd), (r1[1:2, :], bc), (r1[12:13, :], bs), (r3[2:3, :], bmsg)):
                act.dma_start(o, i.rearrange("(a d) -> a d", a=1)).then_inc(S["ld_w"], 16)
            act.dma_start(r3[3:12, :], embed).then_inc(S["ld_w"], 16)
            act.wait_ge(S["q_ssq"], 1)
            nc.scalar.activation(q_s[:, 1:2], q_s[:, 0:1], ACT.Sqrt).then_inc(S["q_norm"], 1)
            for c in range(NCH):
                act.wait_ge(S[f"attr_in{c % 2}"], 32 * (c // 2 + 1))
                if c >= 1:
                    act.wait_ge(S["square_done"], c)
                if c >= 2:
                    act.wait_ge(S["slots_ready"], c - 1)
                for j in range(CT):
                    last = nc.scalar.activation(squa[:, j, :], attr_buf[c % 2][:, j, :], ACT.Square, accum_out=ssq[:, c % 2, j:j + 1])
                last.then_inc(S["square_done"], 1)
                act.wait_ge(S["prod_done"], c + 1)
                for j in range(CT):
                    last = nc.scalar.activation(prod[:, j, :], prod[:, j, :], ACT.Identity, accum_out=dots[:, c % 2, j:j + 1])
                last.then_inc(S["sums_done"], 1)
                if c < 16:
                    if c >= 2:
                        act.wait_ge(S["wt_used"], c - 1)
                    act.dma_start(wtr[:, c % 2, :], wt[:, c * 1024:(c + 1) * 1024]).then_inc(S[f"wt_in{c % 2}"], 16)
                act.wait_ge(S["norm_in"], c + 1)
                nc.scalar.activation(normr[:, c % 2, :], norm2[:, c % 2, :], ACT.Sqrt).then_inc(S["norm_out"], 1)
                if c == 0:
                    act.wait_ge(S["gi"], 1)
                    act.wait_ge(S["gru_ready0"], 1)
                    for k in range(2):
                        nc.scalar.activation(gru[:, k:k + 1], gx[:, k:k + 1], ACT.Sigmoid, bias=gru[:, 6 + k:7 + k]).then_inc(S["gru_rz"], 1)
                    act.wait_ge(S["gru_t"], 1)
                    nc.scalar.activation(gru[:, 4:5], gru[:, 3:4], ACT.Tanh).then_inc(S["gru_n"], 1)

            act.wait_ge(S["row_init"], 1)
            for r in range(GB):
                act.sem_inc(row_out[r], 48)
            act.sem_inc(S["rows_ready"], 4)

            def evacuate(n, piece, g, diagonal):
                for r in range(GB):
                    act.wait_ge(row_out[r], 48 * (n + 1))
                    for h, (lo, hi) in enumerate(((0, 3), (3, 5))):
                        act.wait_ge(S["group_ps"], 10 * n + 2 * r + h + 1)
                        nc.scalar.copy(row_c[0:B, r, :, lo * B:hi * B].rearrange("p m (c n) -> p c m n", n=B),
                                       ps_c[h][:, 0:hi - lo, :, :]).then_inc(S["rows_ready"], 1)
                        nc.scalar.copy(row_s[0:B, r, lo * B:hi * B].rearrange("p (c n) -> p c n", n=B),
                                       ps_s[h][:, 0:hi - lo, :]).then_inc(S["rows_ready"], 1)

            def group_counts(g):
                act.wait_ge(S["counts_ps"], g + 1)
                nc.scalar.copy(countsT[0:F, bass.ds(g * GW, 4 * B)], cnt[0:F, 0:4 * B]).then_inc(S["counts_free"], 1)
                nc.scalar.copy(countsT[0:F, bass.ds(g * GW + 4 * B, B)], gx[0:F, 0:B]).then_inc(S["counts_free"], 1)

            act.sem_inc(S["counts_free"], 2)
            piece_loop(act, evacuate, group_counts)
            def transposed(turn):
                for c in range(7):
                    act.wait_ge(S["t_ready"], turn * 7 + c + 1)
                    lo, hi = c * 4, min(NB, c * 4 + 4)
                    to = countsT if turn == 0 else xT
                    nc.scalar.copy(to[:, lo * B:hi * B], tp[(turn * 7 + c) % 2][0:to.shape[0], 0:(hi - lo) * B]).then_inc(S["t_free"], 1)

            USED = {L0: 0, L1B: G, L2A: 2 * G, L2B: 3 * G, L3: 4 * G}

            def group_out(n, g, to):
                act.wait_ge(S["piece_used"], G * (n * G + g + 1))
                if n != L1A and USED[n] + g > 0:
                    act.wait_ge(S["agg_used"], USED[n] + g)
                for h in range(2):
                    nc.scalar.copy(to[:, h * HALF[0]:h * HALF[0] + HALF[h]], acc[h][:, 0:HALF[h]]).then_inc(S["acc_free"], 1)

            def norm_part(k):
                act.wait_ge(S["xc_ready"], k + 1)
                nc.scalar.activation(sq[:, :, :], yc[:, :, :], ACT.Square).then_inc(S["sq_ready"], 1)
                act.wait_ge(S["sd_in"], k + 1)
                nc.scalar.activation(st[:, 2, :], st[:, 1, :], ACT.Sqrt, bias=epsc[0:B, 0:1], scale=1.0 / D).then_inc(S["sd_ready"], 1)

            transposed(0)
            transposed(1)
            for g in range(G):
                group_out(L0, g, agg)
                norm_part(g)
            for g in range(G):
                group_out(L1A, g, cT[:, g * GW:(g + 1) * GW])
                if g == 0:
                    transposed(2)
            for g in range(G):
                group_out(L1B, g, agg)
                norm_part(G + g)
            for g in range(G):
                group_out(L2A, g, agg)
            for g in range(G):
                group_out(L2B, g, agg)
                norm_part(2 * G + g)

            def finish(g):
                act.wait_ge(S["yt_ready"], g + 1)
                nc.scalar.copy(y[:, 0:4, :], dn[0][0:B, :].rearrange("p (b d) -> p b d", d=D)).then_inc(S["y_ready"], 1)
                nc.scalar.copy(y[:, 4, :], dn[1][0:B, 0:D]).then_inc(S["y_ready"], 1)
                norm_part(3 * G + g)

            for g in range(G):
                group_out(L3, g, agg)
                if g == 0:
                    transposed(3)
                else:
                    finish(g - 1)
                for h in range(2):
                    w, lo = HALF[h], h * HALF[0]
                    act.wait_ge(S["msg_ready"], 2 * g + h + 1)
                    nc.scalar.copy(mT[:, lo:lo + w], dn[h][:, 0:w]).then_inc(S["m_ready"], 1)
                for h in range(2):
                    w, lo = HALF[h], h * HALF[0]
                    act.wait_ge(S["gates_ready"], 2 * g + h + 1)
                    for k in range(2):
                        nc.scalar.activation(gr[:, k, lo:lo + w], tp[k][:, 0:w], ACT.Sigmoid, bias=b3s[:, k:k + 1]).then_inc(S["rz_ready"], 1)
                    act.wait_ge(S["n_in"], 2 * g + h + 1)
                    nc.scalar.activation(gr[:, 2, lo:lo + w], gr[:, 3, lo:lo + w], ACT.Tanh, bias=b3[:, 0, 2:3]).then_inc(S["n_ready"], 1)
            finish(G - 1)

        @block.tensor
        def _(pe):
            pe.sem_inc(S["oh_used"], GB)
            pe.wait_ge(S["consts"], 1)
            for c in range(NCH):
                pe.wait_ge(S["oh_ready"], c + 1)
                for m, w in ((0, before[:, :]), (1, ones_bf[0:B, 0:B])):
                    for j in range(CT):
                        last = nc.tensor.matmul(acc[m][0:B, 0:KEYS], w, oh[:, j, :], start=(j == 0), stop=(j == CT - 1))
                    last.then_inc(S["table_ps0"], 1)
                if c == 0:
                    pe.wait_ge(S["ld_w"], 16 * 19)
                    for k in range(3):
                        last = nc.tensor.matmul(gx[:, k:k + 1], wih0_s[:, k * D:(k + 1) * D], mem_c[:, :], start=True, stop=True)
                    last.then_inc(S["gi"], 1)
                    pe.wait_ge(S["u_ready"], 1)
                if c < 16:
                    pe.wait_ge(S[f"wt_in{c % 2}"], 16 * (c // 2 + 1))
                    for o in range(8):
                        last = nc.tensor.matmul(dn[1][:, c * 8 + o:c * 8 + o + 1], wtr[:, c % 2, o * D:(o + 1) * D], gru[:, 5:6],
                                                start=True, stop=True)
                    last.then_inc(S["wt_used"], 1)
            pe.wait_ge(S["nov_in"], 1)
            nc.tensor.matmul(gx[0:1, 8:9], nov[0:B, 0:1], nov[0:B, 1:2], start=True, stop=True).then_inc(S["nov_ps"], 1)
            pe.wait_ge(S["nw_ready"], 1)

            def clear_counts(stop):
                nc.tensor.matmul(cnt[0:F, 0:4 * B], zrow[0:B, 0:F], zrow[0:B, 0:4 * B], start=not stop, stop=stop, skip_group_check=True)
                return nc.tensor.matmul(gx[0:F, 0:B], zrow[0:B, 0:F], zrow[0:B, 0:B], start=not stop, stop=stop, skip_group_check=True)

            def blocks(n, piece, g, diagonal):
                if diagonal:
                    pe.wait_ge(S["counts_free"], 2 * (g + 1))
                    clear_counts(False)
                for r in range(GB):
                    at, _ = place_of(r)
                    pe.wait_ge(S["oh_full"], GB * n + r + 1)
                    pe.wait_ge(S["ohs_f_ready"], GB * n + r + 1)
                    for c in range(GB):
                        h = c // 3
                        if c % 3 == 0:
                            pe.wait_ge(S["rows_ready"], 20 * n + 4 * r + 2 * h + 2)
                        tiles = tiles_of(r, c, diagonal)
                        to = ps_c[h][:, c - 3 * h, :, :]
                        for t in tiles:
                            first, end = t == tiles[0], t == tiles[-1]
                            nc.tensor.matmul(to.rearrange("p m n -> p (m n)"), ohs[at][:, t, 0:B], ohd[at][:, t, :, 0:B],
                                             start=first, stop=False, skip_group_check=True)
                            nc.tensor.matmul(to[:, 0, :], ohs[at][:, t, 0:B], ohd[at][:, t, 1, 0:B],
                                             start=False, stop=end, skip_group_check=True)
                            last = nc.tensor.matmul(ps_s[h][:, c - 3 * h, :], ohs_f[at][:, t, 0:B], ohsim[at][:, t, 0:B],
                                                    start=first, stop=end, skip_group_check=True)
                            if end and c in (2, 4):
                                last.then_inc(S["group_ps"], 1)
                            src_col = 25 * piece + GB * (g + r) + c if t < GB else GC * g + NB * GB + r
                            for m in range(2):
                                o = cnt[0:F, c * B:(c + 1) * B] if c < 4 else gx[0:F, 0:B]
                                last = nc.tensor.matmul(o, featc[:, bass.ds(src_col, 1), :].rearrange("p a f -> p (a f)"),
                                                        ohd[at][:, t, m, 0:B], start=False, stop=False, skip_group_check=True)
                    last.then_inc(S["oh_used"], 1)

            piece_loop(pe, blocks, lambda g: clear_counts(True).then_inc(S["counts_ps"], 1))
            pe.wait_ge(S["counts_free"], 2 * (G + 1))
            nc.tensor.matmul(cnt[0:B, 0:NB * F], zrow[0:B, 0:B], zrow[0:B, 0:NB * F], start=True, stop=False, skip_group_check=True)
            pe.wait_ge(S["nov_ready"], 1)
            over_n = pe.value_load(nov_i[0:1, 0:1], min_val=0, max_val=E)
            with pe.If(over_n > 0):
                with pe.Fori(0, T) as t:
                    pe.wait_ge(S["tile_ready"], t + 1)
                    nc.tensor.transpose(tp[0][0:B, 0:B], kb[:, :], ident[0:B, 0:B]).then_inc(S["keyrow"], 1)
                    nc.tensor.matmul(cnt[0:B, 0:NB * F], ohoff[:, :], rhs12[:, :, :].rearrange("p b f -> p (b f)"),
                                     start=False, stop=False, skip_group_check=True)
                    pe.wait_ge(S["same_ready"], t + 1)
                    nc.tensor.matmul(tp[1][0:B, 0:3], same[:, :], v3[:, :], start=True, stop=True).then_inc(S["tile_sums"], 1)
            for b in range(NB):
                nc.tensor.matmul(cnt[0:B, b * F:(b + 1) * F], countsT[0:F, b * B:(b + 1) * B], ident[0:F, 0:F],
                                 start=False, stop=False, skip_group_check=True)
            nc.tensor.matmul(cnt[0:B, 0:NB * F], zrow[0:B, 0:B], zrow[0:B, 0:NB * F], start=False, stop=True,
                             skip_group_check=True).then_inc(S["counts_psum"], 1)
            pe.wait_ge(S["rows_ready"], 20 * NPIECE + 4)

            def transposes(turn, xs, chunks=range(7)):
                for c in chunks:
                    if turn * 7 + c >= 2:
                        pe.wait_ge(S["t_free"], turn * 7 + c - 1)
                    for b in range(c * 4, min(NB, c * 4 + 4)):
                        last = nc.tensor.transpose(tp[(turn * 7 + c) % 2][0:xs.shape[2], (b % 4) * B:(b % 4 + 1) * B], xs[0:B, b, :], ident[0:B, 0:B])
                    last.then_inc(S["t_ready"], 1)

            FEATURES = {L0: ("split_ready", 0), L1A: ("split_ready", G), L2A: ("x_ready", G), L2B: ("x2_ready", 0),
                        L3: ("split_ready", 2 * G)}

            def aggregate(n, g, between):
                m, xs = PASSES[n]
                if n * G + g >= 1:
                    pe.wait_ge(S["acc_free"], 2 * (n * G + g))
                if m != SIM:
                    for h in range(2):
                        nc.tensor.matmul(acc[h][:, 0:HALF[h]], zrow[0:B, 0:128], zrow[0:B, 0:HALF[h]], start=True, stop=False,
                                         skip_group_check=True)
                for k in range(G):
                    at = (n * G + g) * G + k
                    if g == 0 and n in FEATURES:
                        name, done = FEATURES[n]
                        pe.wait_ge(S[name], done + k + 1)
                    if m != SIM and k == G - 1:
                        xf = {L0: xa, L1A: xb, L1B: xb, L3: xb}[n]
                        with pe.If(over_n > 0):
                            for s in range(NB):
                                pe.wait_ge(S["over_in"], 16 * ((CPASS[n] * G + g) * NB + s + 1))
                                for h in range(2):
                                    lo = h * HALF[0]
                                    last = nc.tensor.matmul(acc[h][:, 0:HALF[h]], xf[0:B, s, :], obuf[0:B, lo:lo + HALF[h]],
                                                            start=False, stop=False, skip_group_check=True)
                                last.then_inc(S["over_used"], 1)
                    pe.wait_ge(piece_in[at % RING], 16 * (at // RING + 1))
                    for r in range(GB):
                        s = k * GB + r
                        for p3 in range(1 if m == SIM else 3):
                            for h in range(2):
                                lo = r * GW + h * HALF[0]
                                if m == SIM:
                                    last = nc.tensor.matmul(acc[h][:, 0:HALF[h]], xs[0:B, s, :], ring[0:B, at % RING, lo:lo + HALF[h]],
                                                            start=(s == 0), stop=(s == NB - 1))
                                else:
                                    rhs = ring[0:B, at % RING, 0:ROW // 2].bitcast(BF16)[:, lo:lo + HALF[h]]
                                    last = nc.tensor.matmul(acc[h][:, 0:HALF[h]], xs[0:B, p3, s, :], rhs, start=False,
                                                            stop=(s == NB - 1 and p3 == 2), skip_group_check=True)
                    last.then_inc(S["piece_used"], 1)
                    between(k)

            def linear(k, g, terms, bias):
                pe.wait_ge(S["h_ready"], k * G + g + 1)
                if k * G + g >= 1:
                    pe.wait_ge(S["lin_free"], k * G + g)
                for b in range(GB):
                    o = dn[b // 4][0:B, (b % 4) * D:(b % 4 + 1) * D]
                    for i, (lhs, base, w) in enumerate(terms):
                        nc.tensor.matmul(o, lhs[:, (base + b) * B:(base + b + 1) * B], w, start=(i == 0), stop=False)
                    last = nc.tensor.matmul(o, countsT[:, (g * GB + b) * B:(g * GB + b + 1) * B], bias, start=False, stop=True)
                last.then_inc(S["lin_ready"], 1)

            def l0_linear(g):
                linear(0, g, [(hT, 0, nwT[:, :])], r0[:, :])

            def l1_linear(g):
                linear(1, g, [(hT, 0, w1[:, 0, :]), (agg, 0, w1[:, 1, :]), (xT, g * GB, w1[:, 2, :])], r1[:, :])

            def l2_rows(n, g):
                pe.wait_ge(S["acc_free"], 2 * (n * G + g + 1))
                if g or n == L2B:
                    pe.wait_ge(S["tr_free"], (n - L2A) * G + g)
                for b in range(GB):
                    last = nc.tensor.transpose(dn[b // 4][0:B, (b % 4) * D:(b % 4 + 1) * D], agg[:, b * B:(b + 1) * B], ident[:, :])
                last.then_inc(S["tr_ready"], 1)

            def l3_message(g):
                pe.wait_ge(S["acc_free"], 2 * (L3 * G + g + 1))
                if g:
                    pe.wait_ge(S["y_ready"], 2 * g)
                for h in range(2):
                    w, lo = HALF[h], h * HALF[0]
                    nc.tensor.matmul(dn[h][:, 0:w], wmsg_s[:, :], agg[:, lo:lo + w], start=True, stop=False)
                    nc.tensor.matmul(dn[h][:, 0:w], r3[:, :], countsT[:, g * GW + lo:g * GW + lo + w],
                                     start=False, stop=True).then_inc(S["msg_ready"], 1)

            def l3_gates(g, h):
                w, lo = HALF[h], h * HALF[0]
                m, hh = mT[:, lo:lo + w], xT[:, g * GW + lo:g * GW + lo + w]
                pe.wait_ge(S["m_ready"], 2 * g + h + 1)
                if g or h:
                    pe.wait_ge(S["rz_ready"], 2 * (2 * g + h))
                    pe.wait_ge(S["n_in"], 2 * g + h)
                else:
                    pe.wait_ge(S["t_free"], 28)
                for k in range(2):
                    nc.tensor.matmul(tp[k][:, 0:w], wih_s[:, k * D:(k + 1) * D], m, start=True, stop=False)
                    nc.tensor.matmul(tp[k][:, 0:w], whh_s[:, k * D:(k + 1) * D], hh, start=False, stop=True)
                nc.tensor.matmul(gx[:, 0:w], wih_s[:, 2 * D:3 * D], m, start=True, stop=True)
                nc.tensor.matmul(cnt[:, 0:w], whh_s[:, 2 * D:3 * D], hh, start=True, stop=True).then_inc(S["gates_ready"], 1)

            def l3_rows(g):
                pe.wait_ge(S["yT_ready"], 2 * (g + 1))
                for b in range(GB):
                    last = nc.tensor.transpose(dn[b // 4][0:B, (b % 4) * D:(b % 4 + 1) * D], hT[:, b * B:(b + 1) * B], ident[:, :])
                last.then_inc(S["yt_ready"], 1)

            def between(n, g):
                def work_after(k):
                    if n == L0 and g == 0:
                        if k < 2:
                            transposes(0, counts, (range(0, 4), range(4, 7))[k])
                        elif k < 4:
                            transposes(1, xa, (range(0, 4), range(4, 7))[k - 2])
                    elif k == 0 and (n == L0 or n == L1A and g == 0):
                        l0_linear((g - 1) % G)
                    elif n == L1A and g == 1 and k < 2:
                        transposes(2, xb, (range(0, 4), range(4, 7))[k])
                    elif k == 0 and (n == L1B and g or n == L2A and g == 0):
                        l1_linear((g - 1) % G)
                    elif k == 0 and (n in (L2A, L2B) or n == L3 and g == 0):
                        l2_rows(n if g else n - 1, (g - 1) % G)
                    elif n == L3 and g == 1 and k == 0:
                        transposes(3, xb)
                        l3_message(0)
                    elif n == L3 and g:
                        if k == 0:
                            l3_message(g - 1)
                        elif k < 3:
                            l3_gates(g - 1, k - 1)
                        elif k == 4:
                            l3_rows(g - 1)
                return work_after

            pe.wait_ge(S["counts_sb"], 1)
            pe.wait_ge(S["ld_x"], 16)
            for n in range(len(PASSES)):
                for g in range(G):
                    aggregate(n, g, between(n, g))
            l3_message(G - 1)
            for h in range(2):
                l3_gates(G - 1, h)
            l3_rows(G - 1)

        @block.vector
        def _(dve):
            v = nc.vector
            step = Steps(dve, S["dve"])
            step(v.memset(r0[:, :], 0.0))
            step(v.memset(r1[:, :], 0.0))
            step(v.memset(epsc[:, :], EPS))
            v.memset(r3[:, :], 0.0).then_inc(S["w_small"], 1)
            step(v.memset(zrow[:, :], 0.0))
            step(v.memset(ones_bf[:, :], 1.0))
            step(v.memset(base_tab[:, :, :], 0.0))
            step(v.memset(counts[:, :, :], 1.0))
            step(v.memset(nov[:, :], 1.0))
            dve.wait_ge(S["iota_done"], 2)
            step(v.tensor_copy(iot[:, :], iot_i[:, :]))
            step(v.tensor_copy(iota_bf[:, :], iot_i[:, 0:256]))
            lane = iot[:, 256:257]
            step(v.tensor_scalar(ident[:, :], iot[:, 0:128], lane, None, ALU.is_equal))
            step(v.tensor_scalar(before[:, :], iot[0:B, 0:B], lane[0:B], None, ALU.is_gt))
            step(v.tensor_tensor(earlier[:, :, :], iot[0:B, 0:CT].unsqueeze(1).to_broadcast([B, CT, CT]),
                                 iot[0:B, 0:CT].unsqueeze(2).to_broadcast([B, CT, CT]), ALU.is_lt))
            v.tensor_scalar(tri[:, :], iot[:, 0:128], lane, None, ALU.is_lt).then_inc(S["consts"], 1)
            dve.wait_ge(S["ld_edges"], 64)
            dstf, srcf, t2, t9, db, sbl, dg, sk, do, so, key, tmp, key3, caps = ef
            bid, place, more = efx
            for n in range(4):
                step(v.tensor_copy(ef[n], ei[:, n, :]))

            def floor_div(o, i, by, t, mul=1.0, plus=0.0):
                step(v.tensor_scalar(t, i, mul / by, (plus + 0.5) / by - 0.5, ALU.mult, ALU.add))
                step(v.tensor_scalar(o, t, MAGIC, -MAGIC, ALU.add, ALU.add))

            floor_div(db, dstf, B, tmp)
            floor_div(sbl, srcf, B, tmp)
            floor_div(dg, dstf, GW, tmp)
            floor_div(sk, sbl, GB, tmp)
            step(v.scalar_tensor_tensor(do, db, -float(B), dstf, ALU.mult, ALU.add))
            step(v.scalar_tensor_tensor(so, sbl, -float(B), srcf, ALU.mult, ALU.add))
            step(v.scalar_tensor_tensor(key, dg, float(G), sk, ALU.mult, ALU.add))
            step(v.scalar_tensor_tensor(key, key, 128.0, so, ALU.mult, ALU.add))
            step(v.scalar_tensor_tensor(key, key, float(ROW), dstf, ALU.mult, ALU.add))
            step(v.scalar_tensor_tensor(key, dg, -float(GW), key, ALU.mult, ALU.add))
            step(v.scalar_tensor_tensor(tmp, sk, -float(GB), sbl, ALU.mult, ALU.add))
            step(v.scalar_tensor_tensor(key, tmp, float(GW), key, ALU.mult, ALU.add))
            step(v.tensor_scalar(t9, t9, 0.0, 8.0, ALU.max, ALU.min))
            step(v.tensor_scalar(t2, t2, 0.0, None, ALU.not_equal))
            step(v.scalar_tensor_tensor(bid, db, float(NB), sbl, ALU.mult, ALU.add))
            step(v.scalar_tensor_tensor(place, sbl, float(GB), db, ALU.mult, ALU.add))
            step(v.scalar_tensor_tensor(place, dg, float(NB * GB), place, ALU.mult, ALU.add))
            step(v.tensor_scalar(more, sbl, -float(GB), float(NB * GB - LANES * SLOTS), ALU.mult, ALU.add))
            floor_div(winoff[:, 1, :], iot[0:B, 0:NCH], float(NCH), winoff[:, 0, :], float(NB), 13.0)
            d3, p3b = (a.rearrange("p (c j) -> p c j", j=CT) for a in (db, tmp))
            w3 = winoff[:, 1, :].unsqueeze(2).to_broadcast([B, NCH, CT])
            step(v.tensor_tensor(p3b, d3, w3, ALU.subtract))
            step(v.tensor_scalar(tmp, tmp, 1.0, None, ALU.add))
            step(v.scalar_tensor_tensor(key3, tmp, float(NB), sbl, ALU.mult, ALU.add))
            step(v.tensor_tensor(caps, db, sbl, ALU.is_equal))
            step(v.tensor_scalar(caps, caps, 128.0, 128.0, ALU.mult, ALU.add))
            step(v.tensor_scalar(tmp, tmp, 1.0, None, ALU.subtract))
            step(v.tensor_tensor(tmp, tmp, tmp, ALU.mult))
            step(v.tensor_scalar(tmp, tmp, 1.5, -1000.0, ALU.is_gt, ALU.mult))
            step(v.tensor_tensor(caps, caps, tmp, ALU.add))
            step(v.scalar_tensor_tensor(tmp, do, 128.0, so, ALU.mult, ALU.add))
            step(v.tensor_scalar(tmp, tmp, 129.0, None, ALU.add))
            step(v.scalar_tensor_tensor(tmp, t9, 16384.0, tmp, ALU.mult, ALU.add))
            step(v.scalar_tensor_tensor(rec[:, :, 0], t2, 262144.0, tmp, ALU.mult, ALU.add))

            key_c, bid_c, place_c, more_c, caps_c = (a.rearrange("p (c j) -> p c j", j=CT) for a in (key3, bid, place, more, caps))
            sim_c = simv[:, :].rearrange("p (c j) -> p c j", j=CT)
            slot_c = slot[:, :].rearrange("p (c j) -> p c j", j=CT)
            notok_c = notok[:, :].rearrange("p (c j) -> p c j", j=CT)
            rec_c = rec[:, :, 1].rearrange("p (c j) -> p c j", j=CT)

            def one_hot_rows(c):
                v.tensor_tensor(oh[:, :, :], iot[0:B, 0:KEYS].unsqueeze(1).to_broadcast([B, CT, KEYS]),
                                key_c[:, c, :].unsqueeze(2).to_broadcast([B, CT, KEYS]), ALU.is_equal).then_inc(S["oh_ready"], 1)

            def memory_gru():
                dve.wait_ge(S["ld_w"], 16 * 19)
                step(v.tensor_tensor(b3s[:, :], b3[:, 0, :], b3[:, 1, :], ALU.add))
                v.tensor_tensor(gru[:, 6:8], b0[:, 0, 0:2], b0[:, 1, 0:2], ALU.add).then_inc(S["gru_ready0"], 1)
                dve.wait_ge(S["gru_rz"], 2)
                step(v.tensor_tensor(gru[:, 2:3], gru[:, 0:1], b0[:, 1, 2:3], ALU.mult))
                step(v.tensor_tensor(gru[:, 2:3], gru[:, 2:3], b0[:, 0, 2:3], ALU.add))
                v.tensor_tensor(gru[:, 3:4], gru[:, 2:3], gx[:, 2:3], ALU.add).then_inc(S["gru_t"], 1)
                step(v.tensor_scalar(gru[:, 8:9], gru[:, 1:2], -1.0, 1.0, ALU.mult, ALU.add))
                dve.wait_ge(S["gru_n"], 1)
                v.tensor_tensor(gru[:, 5:6], gru[:, 8:9], gru[:, 4:5], ALU.mult).then_inc(S["u_ready"], 1)

            dve.wait_ge(S["ld_q"], 16)
            step(v.tensor_tensor(q_n[:, :], q_bc[:, :], q_bc[:, :], ALU.mult))
            step(v.tensor_reduce(q_s[:, 2:3], q_n[:, :], AXX, ALU.add))
            v.tensor_scalar(q_s[:, 0:1], q_s[:, 2:3], 1e-24, None, ALU.max).then_inc(S["q_ssq"], 1)
            dve.wait_ge(S["q_norm"], 1)
            step(v.reciprocal(q_s[:, 3:4], q_s[:, 1:2]))
            v.tensor_scalar(q_n[:, :], q_bc[:, :], q_s[:, 3:4], None, ALU.mult).then_inc(S["q_ready"], 1)
            dve.wait_ge(S["q_ready"], 1)
            one_hot_rows(0)
            for c in range(NCH):
                dve.wait_ge(S[f"attr_in{c % 2}"], 32 * (c // 2 + 1))
                if c:
                    dve.wait_ge(S["sums_done"], c)
                v.tensor_tensor(prod, attr_buf[c % 2], q_n[:, :].unsqueeze(1).to_broadcast([B, CT, D]), ALU.mult)\
                    .then_inc(S["prod_done"], 1)
                step(v.tensor_tensor(lane_eq[:, :, :], bid_c[:, c, :].unsqueeze(1).to_broadcast([B, CT, CT]),
                                     bid_c[:, c, :].unsqueeze(2).to_broadcast([B, CT, CT]), ALU.is_equal))
                step(v.tensor_tensor(lane_eq[:, :, :], lane_eq[:, :, :], earlier[:, :, :], ALU.mult))
                step(v.tensor_reduce(r_t[:, 0, :], lane_eq[:, :, :], AXX, ALU.add))
                dve.wait_ge(S["square_done"], c + 1)
                v.tensor_scalar(norm2[:, c % 2, :], ssq[:, c % 2, :], 1e-24, None, ALU.max).then_inc(S["norm_in"], 1)
                dve.wait_ge(S["table_ps0"], 2 * (c + 1))
                win = base_tab[:, WIN[c]:WIN[c] + W3, :].rearrange("p a b -> p (a b)")
                step(v.tensor_tensor(table[:, :], acc[0][0:B, 0:KEYS], win, ALU.add))
                step(v.tensor_tensor(win, win, acc[1][0:B, 0:KEYS], ALU.add))
                step(v.tensor_tensor(found, oh[:, :, :], table[:, :].unsqueeze(1).to_broadcast([B, CT, KEYS]), ALU.mult))
                if c + 1 < NCH:
                    one_hot_rows(c + 1)
                step(v.tensor_reduce(r_t[:, 1, :], found, AXX, ALU.add))
                step(v.tensor_tensor(r_t[:, 2, :], r_t[:, 0, :], r_t[:, 1, :], ALU.add))
                step(v.scalar_tensor_tensor(r_t[:, 3, :], r_t[:, 2, :], float(SLOTS), place_c[:, c, :], ALU.mult, ALU.add))
                step(v.scalar_tensor_tensor(r_t[:, 4, :], r_t[:, 2, :], float(LANES), more_c[:, c, :], ALU.is_ge, ALU.mult))
                step(v.tensor_tensor(r_t[:, 5, :], r_t[:, 3, :], r_t[:, 4, :], ALU.add))
                step(v.tensor_tensor(notok_c[:, c, :], r_t[:, 2, :], caps_c[:, c, :], ALU.is_ge))
                step(v.scalar_tensor_tensor(slot_c[:, c, :], notok_c[:, c, :], FAR, r_t[:, 5, :], ALU.mult, ALU.add))
                dve.wait_ge(S["sums_done"], c + 1)
                dve.wait_ge(S["norm_out"], c + 1)
                step(v.reciprocal(r_t[:, 7, :], normr[:, c % 2, :]))
                step(v.tensor_tensor(sim_c[:, c, :], dots[:, c % 2, :], r_t[:, 7, :], ALU.mult))
                v.tensor_copy(rec_c[:, c, :], sim_c[:, c, :]).then_inc(S["slots_ready"], 1)
                if c == 0:
                    memory_gru()
            step(v.tensor_reduce(nov[0:B, 0:1], notok[:, :], AXX, ALU.add))
            v.tensor_copy(nov[0:B, 1:2], ones_bf[0:B, 0:1]).then_inc(S["nov_in"], 1)
            dve.wait_ge(S["nov_ps"], 1)
            v.tensor_copy(nov_i[:, :], gx[0:1, 8:9]).then_inc(S["nov_ready"], 1)
            dve.wait_ge(S["wt_used"], 16)
            v.tensor_tensor(nwT[:, :], dn[1][:, 0:D], wtb_s[:, :], ALU.add).then_inc(S["nw_ready"], 1)

            def split(i, xs, g):
                blk = slice(g * GB, (g + 1) * GB)
                hi, mid, lo = (xs3[i][0:B, n, blk, :] for n in range(3))
                step(v.tensor_copy(hi, xs[0:B, blk, :]))
                step(v.tensor_tensor(sp_t, xs[0:B, blk, :], hi, ALU.subtract))
                step(v.tensor_copy(mid, sp_t))
                v.tensor_tensor(lo, sp_t, mid, ALU.subtract).then_inc(S["split_ready"], 1)
                split_n[0] += 1
                dve.wait_ge(S["split_ready"], split_n[0])

            sp_t = sq[:, :, :]
            split_n = [0]
            dve.wait_ge(S["ld_x"], 16)
            for g in range(G):
                split(0, xa, g)
            dve.wait_ge(S["sums_done"], NCH)
            step(v.memset(row_c.rearrange("p r m n -> p (r m n)"), 0.0))
            v.memset(row_s.rearrange("p r n -> p (r n)"), 0.0).then_inc(S["row_init"], 1)
            dve.wait_ge(S["bucket_in"], 16 * KC)
            dve.wait_ge(S["prefilled"], 16 * (KC + KL))
            w = [work[:, n * SLOTS:(n + 1) * SLOTS] for n in range(4)]
            for n in range(2):
                step(v.tensor_tensor(w[n], bk[0][:, :, n], bk[1][:, :, n], ALU.add))
                for k in range(2, KC):
                    step(v.tensor_tensor(w[n], w[n], bk[k][:, :, n], ALU.add))
            for n in range(2):
                step(v.tensor_copy(early_sum[n], w[n][:, LATE_AT:SLOTS]))

            def unpack(cols, w):
                n = cols.stop - cols.start
                so_f, code_f, do_f, sim_f, t1_f = (fld[:, i, cols] for i in range(5))
                step(v.tensor_copy(sim_f, w[1]))
                step(v.tensor_scalar(t1_f, w[0], 262144.0, None, ALU.is_ge))
                step(v.scalar_tensor_tensor(w[0], t1_f, -262144.0, w[0], ALU.mult, ALU.add))
                floor_div(w[3], w[0], 16384.0, w[1])
                step(v.scalar_tensor_tensor(w[0], w[3], -16384.0, w[0], ALU.mult, ALU.add))
                floor_div(w[2], w[0], 128.0, w[1])
                step(v.scalar_tensor_tensor(w[0], w[2], -128.0, w[0], ALU.mult, ALU.add))
                step(v.tensor_scalar(so_f, w[0], 1.0, None, ALU.subtract))
                step(v.tensor_scalar(do_f, w[2], 1.0, None, ALU.subtract))
                step(v.scalar_tensor_tensor(code_f, t1_f, 128.0, do_f, ALU.mult, ALU.add))
                step(v.tensor_scalar(featc[:, cols, 0], t1_f, 0.0, None, ALU.is_equal))
                step(v.tensor_copy(featc[:, cols, 1], t1_f))
                step(v.memset(featc[:, cols, 2], 1.0))
                step(v.tensor_tensor(featc[:, cols, 3:12], w[3].unsqueeze(2).to_broadcast([128, n, 9]),
                                     iot[:, 0:9].unsqueeze(1).to_broadcast([128, n, 9]), ALU.is_equal))

            unpack(slice(0, LATE_AT), [a[:, 0:LATE_AT] for a in w])

            def one_hots(n, piece, g, diagonal):
                v.tensor_scalar(fb[:, :, 0:25], fld[:, 0:4, bass.ds(25 * piece + GB * g, 25)], 1.0, None, ALU.mult).then_inc(S["fields_ready"], 1)
                if diagonal:
                    v.tensor_scalar(fb[:, :, 25:30], fld[:, 0:4, bass.ds(GC * g + NB * GB, GB)], 1.0, None, ALU.mult).then_inc(S["fields_ready"], 1)
                dve.wait_ge(S["fields_ready"], n + g + 2)
                for r in range(GB):
                    at, ago = place_of(r)
                    dve.wait_ge(S["oh_used"], GB * n + r + GB + 1 - ago)
                    last = v.tensor_tensor(ohs[at][:, 0:GB, 0:B], iota_bf[:, 0:B].unsqueeze(1).to_broadcast([128, GB, B]),
                                           fb[:, 0, GB * r:GB * r + GB].unsqueeze(2).to_broadcast([128, GB, B]), ALU.is_equal)
                    if diagonal:
                        last = v.tensor_scalar(ohs[at][:, GB, 0:B], iota_bf[:, 0:B], fb[:, 0, 25 + r:26 + r], None, ALU.is_equal)
                    last.then_inc(S["ohs_ready"], 1)
                    for t in range(GB + diagonal):
                        col = GB * r + t if t < GB else 25 + r
                        v.tensor_scalar(ohd[at][:, t, :, :].rearrange("p m n -> p (m n)"), iota_bf[:, :], fb[:, 1, col:col + 1],
                                        None, ALU.is_equal)
                        last = v.tensor_scalar(ohsim[at][:, t, 0:B], iota_bf[:, 0:B], fb[:, 2, col:col + 1],
                                               fb[:, 3, col:col + 1], ALU.is_equal, ALU.mult)
                    last.then_inc(S["oh_full"], 1)
                dve.wait_ge(S["oh_full"], GB * n + GB)
                v.memset(mark2[:, :], 0.0)

            piece_loop(dve, one_hots, groups=(0, LG))
            dve.wait_ge(S["late_back"], 16 * KL)
            for n in range(2):
                step(v.tensor_tensor(late_w[n], early_sum[n], late_in[0][:, :, n], ALU.add))
                for k in range(1, KL):
                    step(v.tensor_tensor(late_w[n], late_w[n], late_in[k][:, :, n], ALU.add))
            unpack(slice(LATE_AT, SLOTS), late_w)
            piece_loop(dve, one_hots, groups=(LG, G))

            dve.wait_ge(S["nov_ready"], 1)
            over_n = dve.value_load(nov_i[0:1, 0:1], min_val=0, max_val=E)
            with dve.If(over_n > 0):
                fb_step = Steps(dve, S["fbv"])
                fb_step(v.tensor_scalar(key, key, 1.0, None, ALU.add))
                fb_step(v.tensor_tensor(key, key, notok[:, :], ALU.mult))
                fb_step(v.tensor_scalar(key, key, 1.0, None, ALU.subtract))
                dve.wait_ge(S["tile_done"], 1)
                with dve.Fori(0, T) as t:
                    n_ = [0]

                    def lk(ins):
                        n_[0] += 1
                        ins.then_inc(S["fbv"], 1)
                        dve.wait_ge(S["fbv"], 3 + 13 * t + n_[0])

                    at = bass.ds(t, 1)
                    v.tensor_copy(kcol[:, 0:1], key[:, at])
                    v.tensor_copy(kcol[:, 1:2], notok[:, at])
                    v.tensor_scalar(ohoff[:, :], iota_bf[0:B, 0:B], do[:, at], None, ALU.is_equal)
                    v.tensor_copy(frow[:, 1:2], t2[:, at])
                    lk(v.tensor_scalar(frow[:, 3:12], iot[0:B, 0:9], t9[:, at], None, ALU.is_equal))
                    v.tensor_scalar(frow[:, 0:1], frow[:, 1:2], 0.0, None, ALU.is_equal)
                    lk(v.memset(frow[:, 2:3], 1.0))
                    v.tensor_copy(v3[:, 0:1], kcol[:, 1:2])
                    v.tensor_tensor(v3[:, 1:2], kcol[:, 1:2], frow[:, 1:2], ALU.mult)
                    v.tensor_tensor(v3[:, 2:3], kcol[:, 1:2], simv[:, at], ALU.mult)
                    lk(v.tensor_scalar(ohdb[:, :], iot[0:B, 0:NB], db[:, at], kcol[:, 1:2], ALU.is_equal, ALU.mult))
                    lk(v.tensor_tensor(rhs12[:, :, :], ohdb[:, :].unsqueeze(2).to_broadcast([B, NB, F]),
                                       frow[:, :].unsqueeze(1).to_broadcast([B, NB, F]), ALU.mult))
                    v.tensor_scalar(kb[:, :], key[:, at].to_broadcast([B, B]), 1.0, None, ALU.mult).then_inc(S["tile_ready"], 1)
                    dve.wait_ge(S["keyrow"], t + 1)
                    lk(v.tensor_scalar(same[:, :], tp[0][0:B, 0:B], kcol[:, 0:1], None, ALU.is_equal))
                    v.tensor_tensor(same_tri[:, :], same[:, :], tri[0:B, 0:B], ALU.mult).then_inc(S["same_ready"], 1)
                    dve.wait_ge(S["same_ready"], t + 1)
                    lk(v.tensor_reduce(rank1[:, :], same_tri[:, :], AXX, ALU.add))
                    lk(v.tensor_scalar(kcol[:, 2:3], kcol[:, 0:1], 0.0, None, ALU.is_lt))
                    lk(v.tensor_tensor(kcol[:, 2:3], kcol[:, 2:3], rank1[:, :], ALU.add))
                    lk(v.tensor_scalar(kcol[:, 2:3], kcol[:, 2:3], 1.0, None, ALU.min))
                    lk(v.scalar_tensor_tensor(kcol[:, 3:4], kcol[:, 0:1], -1.0, lane[0:B], ALU.mult, ALU.add))
                    lk(v.tensor_scalar(kcol[:, 3:4], kcol[:, 3:4], float(ELEMS), None, ALU.add))
                    lk(v.tensor_tensor(kcol[:, 3:4], kcol[:, 3:4], kcol[:, 2:3], ALU.mult))
                    lk(v.tensor_tensor(idx[:, :], kcol[:, 3:4], kcol[:, 0:1], ALU.add))
                    assert n_[0] == 13
                    dve.wait_ge(S["tile_sums"], t + 1)
                    v.tensor_copy(s3[:, :], tp[1][0:B, 0:3]).then_inc(S["idx_ready"], 1)
                    dve.wait_ge(S["tile_done"], t + 2)
                    for m in range(3):
                        dve.wait_ge(oscat[m], 16 * (t + 1))
            dve.wait_ge(S["counts_psum"], 1)
            v.tensor_copy(counts[:, :, 0:F], cnt[0:B, 0:NB * F].rearrange("p (b f) -> p b f", f=F)).then_inc(S["counts_sb"], 1)
            dve.wait_ge(S["counts_sb"], 1)
            step(v.tensor_scalar(halfdeg[:, :], counts[:, :, 2], 1.0, None, ALU.max))
            step(v.reciprocal(halfdeg[:, :], halfdeg[:, :]))
            step(v.tensor_scalar(halfdeg[:, :], halfdeg[:, :], 0.5, None, ALU.mult))

            def layernorm(k, g, xo):
                step(v.tensor_reduce(st[:, 0, :], y[:, :, :], AXX, ALU.add))
                step(v.tensor_scalar(st[:, 0, :], st[:, 0, :], 1.0 / D, None, ALU.mult))
                v.tensor_tensor(yc[:, :, :], y[:, :, :], st[:, 0, :].unsqueeze(2).to_broadcast([B, GB, D]), ALU.subtract)\
                    .then_inc(S["xc_ready"], 1)
                dve.wait_ge(S["sq_ready"], k * G + g + 1)
                v.tensor_reduce(st[:, 1, :], sq[:, :, :], AXX, ALU.add).then_inc(S["sd_in"], 1)
                dve.wait_ge(S["sd_ready"], k * G + g + 1)
                step(v.reciprocal(st[:, 3, :], st[:, 2, :]))
                v.tensor_tensor(xo[0:B, g * GB:(g + 1) * GB, :], yc[:, :, :], st[:, 3, :].unsqueeze(2).to_broadcast([B, GB, D]),
                                ALU.mult).then_inc(S["x_ready"], 1)
                dve.wait_ge(S["x_ready"], k * G + g + 1)

            def relu_add(k, g, xs):
                dve.wait_ge(S["lin_ready"], k * G + g + 1)
                v.scalar_tensor_tensor(y[:, 0:4, :], dn[0][0:B, :].rearrange("p (b d) -> p b d", d=D), 0.0,
                                       xs[0:B, g * GB:g * GB + 4, :], ALU.max, ALU.add)
                v.scalar_tensor_tensor(y[:, 4, :], dn[1][0:B, 0:D], 0.0, xs[0:B, g * GB + 4, :], ALU.max, ALU.add)\
                    .then_inc(S["lin_free"], 1)
                dve.wait_ge(S["lin_free"], k * G + g + 1)

            for g in range(G):
                dve.wait_ge(S["acc_free"], 2 * (L0 * G + g + 1))
                dve.wait_ge(S["t_free"], 14)
                v.tensor_tensor(hT[:, :], agg[:, :], xT[:, g * GW:(g + 1) * GW], ALU.add).then_inc(S["h_ready"], 1)
                dve.wait_ge(S["h_ready"], g + 1)
                dve.sem_inc(S["agg_used"], 1)
                relu_add(0, g, xa)
                layernorm(0, g, xb)
                split(1, xb, g)
            for g in range(G):
                dve.wait_ge(S["acc_free"], 2 * (L1B * G + g + 1))
                dve.wait_ge(S["t_free"], 21)
                v.tensor_tensor(hT[:, :], cT[:, g * GW:(g + 1) * GW], agg[:, :], ALU.subtract).then_inc(S["h_ready"], 1)
                relu_add(1, g, xb)
                dve.sem_inc(S["agg_used"], 1)
                layernorm(1, g, xc)

            def mix(n, g, xs, to):
                dve.wait_ge(S["tr_ready"], (n - L2A) * G + g + 1)
                hd = halfdeg[:, g * GB:(g + 1) * GB].unsqueeze(2)
                v.tensor_tensor(yc[:, 0:4, :], dn[0][0:B, :].rearrange("p (b d) -> p b d", d=D),
                                hd[:, 0:4, :].to_broadcast([B, 4, D]), ALU.mult)
                v.tensor_tensor(yc[:, 4:5, :], dn[1][0:B, 0:D].unsqueeze(1), hd[:, 4:5, :].to_broadcast([B, 1, D]), ALU.mult)\
                    .then_inc(S["tr_free"], 1)
                dve.wait_ge(S["tr_free"], (n - L2A) * G + g + 1)
                dve.sem_inc(S["agg_used"], 1)
                step(v.scalar_tensor_tensor(to, xs[0:B, g * GB:(g + 1) * GB, :], 0.5, yc[:, :, :], ALU.mult, ALU.add))

            for g in range(G):
                mix(L2A, g, xc, xa[0:B, g * GB:(g + 1) * GB, :])
                dve.sem_inc(S["x2_ready"], 1)
            for g in range(G):
                mix(L2B, g, xa, y[:, :, :])
                step(v.tensor_tensor(y[:, :, :], y[:, :, :], xc[0:B, g * GB:(g + 1) * GB, :], ALU.add))
                layernorm(2, g, xb)
                split(0, xb, g)
            for g in range(G):
                for h in range(2):
                    w, lo = HALF[h], h * HALF[0]
                    r, z, n_, t_ = (gr[:, k, lo:lo + w] for k in range(4))
                    xx = xT[:, g * GW + lo:g * GW + lo + w]
                    yy = hT[:, lo:lo + w]
                    dve.wait_ge(S["gates_ready"], 2 * g + h + 1)
                    dve.wait_ge(S["rz_ready"], 2 * (2 * g + h + 1))
                    step(v.scalar_tensor_tensor(t_, cnt[:, 0:w], b3[:, 1, 2:3], r, ALU.add, ALU.mult))
                    v.tensor_tensor(t_, t_, gx[:, 0:w], ALU.add).then_inc(S["n_in"], 1)
                    dve.wait_ge(S["n_ready"], 2 * g + h + 1)
                    if g and not h:
                        dve.wait_ge(S["yt_ready"], g)
                    step(v.tensor_tensor(yy, xx, n_, ALU.subtract))
                    step(v.tensor_tensor(yy, yy, z, ALU.mult))
                    step(v.tensor_tensor(yy, yy, n_, ALU.add))
                    v.tensor_tensor(yy, yy, xx, ALU.add).then_inc(S["yT_ready"], 1)
                dve.wait_ge(S["msg_ready"], 2 * (g + 1))
                dve.sem_inc(S["agg_used"], 1)
                dve.wait_ge(S["y_ready"], 2 * (g + 1))
                layernorm(3, g, xa)



_INS = ['x', 'src', 'dst', 'edge_attr_128', 'edge_type_2', 'edge_type_9', 'L0_gnn_memory', 'L0_gnn_gru_w_ih',
        'L0_gnn_gru_b_ih', 'L0_gnn_gru_b_hh', 'L0_gnn_wt_w', 'L0_gnn_wt_b', 'L0_gnn_lin_b', 'L1_gnn_W_data',
        'L1_gnn_b_data', 'L1_gnn_W_control', 'L1_gnn_b_control', 'L1_gnn_W_self', 'L1_gnn_b_self',
        'L2_gnn_question_emb', 'L3_gnn_W_msg', 'L3_gnn_b_msg', 'L3_gnn_edge_embed', 'L3_gnn_W_ih', 'L3_gnn_W_hh',
        'L3_gnn_b_ih', 'L3_gnn_b_hh']


def kernel(**inputs):
    import numpy as _np
    import concourse.bacc as _bacc
    from concourse import mybir as _mybir
    from concourse.bass_utils import run_bass_kernel_spmd as _run

    def lay(name, a):
        if name == 'L0_gnn_wt_b':
            return a.reshape(D, D).T
        if 'gru_b' in name or name in ('L3_gnn_b_ih', 'L3_gnn_b_hh'):
            return a.reshape(3, D).T
        if '_W_' in name or '_w_ih' in name or name in ('L0_gnn_memory', 'L0_gnn_wt_w'):
            return a.T
        return a

    nc = _bacc.Bacc("TRN2", target_bir_lowering=False, num_devices=1)
    arrays, args = {}, []
    for name in _INS:
        a = _np.ascontiguousarray(lay(name, _np.asarray(inputs[name])))
        arrays[f"in_{name}"] = a
        args.append(nc.dram_tensor(f"in_{name}", a.shape, _mybir.dt.from_np(a.dtype), kind="ExternalInput").ap())
    args.append(nc.dram_tensor("out_0", (N, D), _mybir.dt.float32, kind="ExternalOutput").ap())
    program(nc, *args)
    r = _run(nc, [arrays], core_ids=[0])
    return r.results[0]["out_0"]
```
